# Optimizing a Trainium2 kernel written in Bass

```python
import numpy as np
import jax
import jax.numpy as jnp

def _softmax(x, axis=-1):
    return jax.nn.softmax(x, axis=axis)

def _gelu(x):
    return jax.nn.gelu(x, approximate=True)

def _silu(x):
    return jax.nn.silu(x)

def _sigmoid(x):
    return jax.nn.sigmoid(x)

def _layernorm(x, axis=-1, eps=1e-05):
    m = jnp.mean(x, axis=axis, keepdims=True)
    v = jnp.var(x, axis=axis, keepdims=True)
    return (x - m) / jnp.sqrt(v + eps)

def _scatter_add(tgt, idx, src, axis=0):
    return tgt.at[idx].add(src)

def _segment_sum(src, seg, n):
    return jax.ops.segment_sum(src, seg, n)
kernel_name = 'mk_macaron_d1_jaxref_r8_1eaaf5'

def setup_inputs(seed: int=0):
    np.random.seed(seed)
    _w = jnp.asarray

    def _L0_attn_setup():
        import jax, jax.numpy as jnp
        import numpy as np
        key = jax.random.key(seed)
        ks = jax.random.split(key, 5)
        Bsz, T, d = (8, 256, 128)
        x = jax.random.normal(ks[0], (Bsz, T, d), dtype=jnp.float32)
        W_in = jax.random.normal(ks[1], (d, d), dtype=jnp.float32) * (1.0 / np.sqrt(d))
        b_in = jnp.zeros((d,), dtype=jnp.float32)
        log_A = -jnp.ones((d,), dtype=jnp.float32)
        B_vec = jax.random.normal(ks[2], (d,), dtype=jnp.float32) * 0.05
        C = jax.random.normal(ks[3], (d, d), dtype=jnp.float32) * 0.05
        D = jnp.zeros((d,), dtype=jnp.float32)
        return {'x': x, 'W_in': W_in, 'b_in': b_in, 'log_A': log_A, 'B_vec': B_vec, 'C': C, 'D': D}
    _L0_attn_in = _L0_attn_setup()

    def _L0_ffn_setup():
        import jax, jax.numpy as jnp
        import numpy as np
        NUM_EXPERTS = 8
        EXPERT_CAPACITY = 2.0
        key = jax.random.key(seed)
        k1, k2, k3, k4 = jax.random.split(key, 4)
        B, T, C, H, E = (4, 512, 128, 512, NUM_EXPERTS)
        x = jax.random.normal(k1, (B, T, C), jnp.float32)
        gate_w = jax.random.normal(k2, (C, E), jnp.float32) * 0.02
        w1 = jax.random.normal(k3, (E, C, H), jnp.float32) * 0.02
        w2 = jax.random.normal(k4, (E, H, C), jnp.float32) * 0.02
        return {'x': x, 'gate_w': gate_w, 'w1': w1, 'w2': w2}
    _L0_ffn_in = _L0_ffn_setup()
    _d = {'L0_attn_x': _L0_attn_in['x'], 'L0_attn_W_in': _L0_attn_in['W_in'], 'L0_attn_b_in': _L0_attn_in['b_in'], 'L0_attn_log_A': _L0_attn_in['log_A'], 'L0_attn_B_vec': _L0_attn_in['B_vec'], 'L0_attn_C': _L0_attn_in['C'], 'L0_attn_D': _L0_attn_in['D'], 'L0_ffn_gate_w': _L0_ffn_in['gate_w'], 'L0_ffn_w1': _L0_ffn_in['w1'], 'L0_ffn_w2': _L0_ffn_in['w2']}
    _x0 = _d['L0_attn_x']
    _d['L0_attn_x'] = jax.random.normal(jax.random.fold_in(jax.random.key(seed), 1), (16, 256, 128), dtype=_x0.dtype)
    del _x0
    return _d

def reference(L0_attn_x, L0_attn_W_in, L0_attn_b_in, L0_attn_log_A, L0_attn_B_vec, L0_attn_C, L0_attn_D, L0_ffn_gate_w, L0_ffn_w1, L0_ffn_w2):

    def _L0_attn_ref(x, W_in, b_in, log_A, B_vec, C, D):
        import jax, jax.numpy as jnp
        import numpy as np
        u = jnp.einsum('btd,de->bte', x, W_in) + b_in
        A = -jnp.exp(log_A)
        b = u * B_vec
        a = jnp.broadcast_to(A, b.shape)

        def combine(e1, e2):
            a1, b1 = e1
            a2, b2 = e2
            return (a1 * a2, b1 * a2 + b2)
        _, h_seq = jax.lax.associative_scan(combine, (a, b), axis=1)
        y = jnp.einsum('bts,sd->btd', h_seq, C)
        return y + x * D

    def _L0_ffn_ref(x, gate_w, w1, w2):
        import jax, jax.numpy as jnp
        import numpy as np
        NUM_EXPERTS = 8
        EXPERT_CAPACITY = 2.0
        B, T, C = x.shape
        E = gate_w.shape[1]
        cap = int(EXPERT_CAPACITY * T / E)
        scores = jnp.einsum('BTC,CE->BTE', x, gate_w)
        probs = jax.nn.softmax(scores, axis=-1)
        probs_et = jnp.transpose(probs, (0, 2, 1))
        top_p, top_idx = jax.lax.top_k(probs_et, cap)
        xin = jnp.take_along_axis(x[:, None, :, :], top_idx[..., None], axis=2)
        h = jax.nn.gelu(jnp.einsum('BElC,ECH->BElH', xin, w1), approximate=False)
        y = jnp.einsum('BElH,EHC->BElC', h, w2)
        y = y * top_p[..., None]
        b_idx = jnp.arange(B)[:, None, None]
        out = jnp.zeros((B, T, C), x.dtype).at[b_idx, top_idx].add(y)
        return out
    x = L0_attn_x
    x = x + 0.5 * _L0_ffn_ref(_layernorm(x, axis=-1), L0_ffn_gate_w, L0_ffn_w1, L0_ffn_w2)
    x = x + _L0_attn_ref(_layernorm(x, axis=-1), L0_attn_W_in, L0_attn_b_in, L0_attn_log_A, L0_attn_B_vec, L0_attn_C, L0_attn_D)
    x = x + 0.5 * _L0_ffn_ref(_layernorm(x, axis=-1), L0_ffn_gate_w, L0_ffn_w1, L0_ffn_w2)
    return x

_drawn_inputs = setup_inputs


def setup_inputs(seed=0):
    import zlib

    import numpy as np

    out = dict(_drawn_inputs(seed))
    spreads = {'L0_attn_b_in': (0.0, 2.0), 'L0_attn_log_A': (-1.0, 0.6), 'L0_attn_D': (0.0, 0.1)}
    factors = {'L0_ffn_gate_w': 5.288, 'L0_ffn_w1': 4.719, 'L0_ffn_w2': 4.641}
    for name, (base, spread) in spreads.items():
        noise = np.random.default_rng([zlib.crc32(name.encode()), seed]).standard_normal(out[name].shape)
        drawn = base * np.exp(spread * noise) if base else spread * noise
        out[name] = jnp.asarray(drawn.astype(out[name].dtype))
    for name, factor in factors.items():
        out[name] = (out[name] * factor).astype(out[name].dtype)
    return out
```

```python
import numpy as np
from contextlib import ExitStack, contextmanager

import concourse.bass as bass
from concourse import mybir

FP32 = mybir.dt.float32
FP16 = mybir.dt.float16
INT32 = mybir.dt.int32
UINT32 = mybir.dt.uint32
ALU = mybir.AluOpType
ACT = mybir.ActivationFunctionType
AX = mybir.AxisListType


class Chain:

    def __init__(self, eng, sem):
        self.eng, self.sem = eng, sem
        self.base, self.local, self.offset = 0, 0, 0

    def link(self, instruction):
        instruction.then_inc(self.sem, 1)
        self.local += 1
        self.eng.wait_ge(self.sem, self.offset + self.base + self.local)

    @contextmanager
    def loop(self, start, end, links):
        self.base, self.local = self.base + self.local, 0
        with self.eng.Fori(start, end) as i:
            self.offset = i * links
            self.base -= start * links
            yield i
            assert self.local == links, (self.local, links)
            self.base += start * links
        self.base, self.local, self.offset = self.base + (end - start) * links, 0, 0


def macaron_kernel(nc, x_d, w_in_d, b_in_d, log_a_d, b_vec_d, c_d, d_d, gate_d, w1_d, w2_d, out_d):
    B, T, C = x_d.shape
    E, _, H = w1_d.shape
    P = 128
    TH = T // P
    CAP = 2 * T // E
    HB = B // 2
    NPH = 4
    NCH = 4
    CB = HB // NCH
    CT = CB * TH
    HT = HB * TH
    PAIRS = E // 2
    HC = H // P
    UNITS = 2 * PAIRS * 2
    SLOTS = HB * CAP
    ROUNDS = CAP // 8
    assert C == P and SLOTS == 512 and 2 * CAP == P and HC == 4 and NCH == PAIRS
    EPS = 1e-5
    LN_SCALE = 2.0 ** 10
    W_TOP = 2.0 ** 13
    Y_SCALE = 2.0 ** -23
    EXP_BITS = 0x7F800000

    ctx = ExitStack()
    with ctx:
        def sb(name, shape, dt=FP32):
            return ctx.enter_context(nc.sbuf_tensor(name, shape, dt))

        def sem(name):
            return ctx.enter_context(nc.semaphore(name))

        x = sb("x", [P, B * TH, C])
        w1f = sb("w1f", [P, E, H])
        w2f = sb("w2f", [P, E, HC, C])
        w1s = sb("w1s", [P, 2, E, H], FP16)
        w2s = sb("w2s", [P, 2, E, HC, C], FP16)
        gwf = sb("gwf", [P, E])
        gws = sb("gws", [P, 2, E], FP16)
        w_in = sb("w_in", [P, P])
        c_mat = sb("c_mat", [P, P])
        d_row = sb("d_row", [P, C])
        b_in = sb("b_in", [P, 1])
        b_vec = sb("b_vec", [P, 1])
        log_a = sb("log_a", [P, 1])
        exp_a = sb("exp_a", [P, 1])
        decay = sb("decay", [P, T])
        ident = sb("ident", [P, P])
        ident16 = sb("ident16", [P, P], FP16)
        iota = sb("iota", [P, T], FP16)
        half_neg = sb("half_neg", [P, CT])
        amax = sb("amax", [P, 4])
        amax_all = sb("amax_all", [P, 4])
        pow2 = sb("pow2", [P, 4])
        scale = sb("scale", [P, 4])
        gelu_scale = sb("gelu_scale", [P, 1])
        h_scale = sb("h_scale", [P, 1])
        exp_scale = sb("exp_scale", [P, 1])
        out_scale = sb("out_scale", [P, 1])

        mean = sb("mean", [P, CT])
        squares = sb("squares", [P, CT, C])
        var_eps = sb("var_eps", [P, CT])
        rstd = sb("rstd", [P, CT])
        mean_a = sb("mean_a", [P, CT])
        var_eps_a = sb("var_eps_a", [P, CT])
        rstd_a = sb("rstd_a", [P, CT])
        zf = sb("zf", [P, CT, C])
        xn = sb("xn", [P, 2, HT, C], FP16)
        xt = sb("xt", [P, CT, 2, P], FP16)
        za = sb("za", [P, CT, C])
        zd = sb("zd", [P, CT, C])
        zt = sb("zt", [P, CT * P])
        bt = sb("bt", [P, CT * P])
        hseq = sb("hseq", [P, CT * P])

        smax = sb("smax", [P, HT])
        sdiff = sb("sdiff", [P, HT, E])
        sexp = sb("sexp", [P, HT, E])
        ssum = sb("ssum", [P, HT])
        srec = sb("srec", [P, HT])
        probs = sb("probs", [P, HT, E])
        RW = HB * E
        ranked = sb("ranked", [RW, 2, T])
        top = sb("top", [RW, CAP])
        idx = sb("idx", [RW, CAP], UINT32)
        top2 = sb("top2", [RW, 2, CAP])
        idx2 = sb("idx2", [RW, 2, CAP])
        idx_s = sb("idx_s", [P, PAIRS, HB])
        top_s = sb("top_s", [P, PAIRS, HB])

        onehot = sb("onehot", [P, HB, PAIRS, T], FP16)
        onehot_t = sb("onehot_t", [P, 2, TH, PAIRS * P], FP16)
        xin = sb("xin", [P, 2, E, HB, CAP], FP16)
        hf = sb("hf", [P, 2, 2 * SLOTS])
        hs = sb("hs", [P, 4, 2, 2 * SLOTS], FP16)
        yt = sb("yt", [P, HB, 2, CAP])
        yf = sb("yf", [P, 2, 4, C])
        ys = sb("ys", [P, 2, HB, PAIRS, C], FP16)

        ps = ctx.enter_context(nc.psum_tensor("ps", [P, 8, 512], FP32))
        Y_BANK, TY_BANK, SIDE_BANK, SCORE_BANK = 4, 5, 6, 7
        side = ps[:, SIDE_BANK, :]
        side16 = side.bitcast(FP16).rearrange("p (t s c) -> p t s c", t=CT, s=2)
        score = ps[:, SCORE_BANK, 0:HT * E].rearrange("p (h b e) -> p h b e", h=TH, e=E)

        x_in = [sem(f"x_in{h}") for h in range(2)]
        gate_in, w1_in, w2_in, att_in = sem("gate_in"), sem("w1_in"), sem("w2_in"), sem("att_in")
        consts = sem("consts")
        amax_ready, amax_shared = sem("amax_ready"), sem("amax_shared")
        scales_ready, w_high, w_split = sem("scales_ready"), sem("w_high"), sem("w_split")
        gate_high, gate_split = sem("gate_high"), sem("gate_split")
        loga_exp, decay_ready = sem("loga_exp"), sem("decay_ready")
        dve_chain, act_chain, pool_chain = sem("dve_chain"), sem("act_chain"), sem("pool_chain")
        ln_var, ln_rstd, xn_ready = sem("ln_var"), sem("ln_rstd"), sem("xn_ready")
        xt_ready, xt_copied, scored = sem("xt_ready"), sem("xt_copied"), sem("scored")
        sdiff_ready, sexp_ready, probs_ready = sem("sdiff_ready"), sem("sexp_ready"), sem("probs_ready")
        pt_turned, topk_ready, topk_turned = sem("pt_turned"), sem("topk_ready"), sem("topk_turned")
        onehot_ready, turned, turned_copied = sem("onehot_ready"), sem("turned"), sem("turned_copied")
        gathered, high_copied, low_copied = sem("gathered"), sem("high_copied"), sem("low_copied")
        up_done, gelu_done, h_high, h_low = sem("up_done"), sem("gelu_done"), sem("h_high"), sem("h_low")
        down_done, y_copied = sem("down_done"), sem("y_copied")
        y_turned, y_weighed, y_split = sem("y_turned"), sem("y_weighed"), sem("y_split")
        scattered, x_updated = sem("scattered"), sem("x_updated")
        att_var, att_rstd, z_ready, xd_added = sem("att_var"), sem("att_rstd"), sem("z_ready"), sem("xd_added")
        zt_ready, zt_copied, u_ready = sem("zt_ready"), sem("zt_copied"), sem("u_ready")
        hseq_ready, v_ready, v_added = sem("hseq_ready"), sem("v_ready"), sem("v_added")
        out_sent = sem("out_sent")

        CREDIT = 2

        def tiles_of(half, i):
            return bass.ds(half * HT + i * CT, CT) if not isinstance(i, int) else slice(half * HT + i * CT, half * HT + (i + 1) * CT)

        def at(i, n):
            return bass.ds(i, n) if not isinstance(i, int) else slice(i, i + n)

        block = ctx.enter_context(nc.Block())

        @block.sync
        def _(sp):
            xv = x_d.rearrange("b (h p) c -> p (b h) c", p=P)
            ov = out_d.rearrange("b (h p) c -> p (b h) c", p=P)
            q = HT // 2
            for k in range(2):
                sp.dma_start(x[:, k * q:(k + 1) * q, :], xv[:, k * q:(k + 1) * q, :]).then_inc(x_in[0], 16)
            sp.dma_start(gwf[:, :], gate_d).then_inc(gate_in, 16)
            sp.dma_start(w1f[:, :, :], w1_d.rearrange("e c h -> c e h")).then_inc(w1_in, 16)
            sp.dma_start(w2f[:, :, :, :], w2_d.rearrange("e (k p) c -> p e k c", p=P)).then_inc(w2_in, 16)
            sp.dma_start(x[:, HT:2 * HT, :], xv[:, HT:2 * HT, :]).then_inc(x_in[1], 16)
            sp.dma_start(w_in[:, :], w_in_d).then_inc(att_in, 16)
            sp.dma_start(c_mat[:, :], c_d).then_inc(att_in, 16)
            sp.dma_start(d_row[:, :], d_d.rearrange("(a c) -> a c", a=1).broadcast_to([P, C])).then_inc(att_in, 16)
            for dst, src in ((b_in, b_in_d), (b_vec, b_vec_d), (log_a, log_a_d)):
                sp.dma_start(dst[:, :], src.rearrange("(c a) -> c a", a=1)).then_inc(att_in, 16)
            for half in range(2):
                for k in range(2):
                    lo = half * HT + k * q
                    sp.wait_ge(x_updated, CREDIT + (2 + half) * HB + (k + 1) * HB // 2)
                    sp.dma_start(ov[:, lo:lo + q, :], x[:, lo:lo + q, :]).then_inc(out_sent, 16)
            sp.wait_ge(out_sent, 4 * 16)

        @block.gpsimd
        def _(pool):
            chain = Chain(pool, pool_chain)
            chain.link(nc.gpsimd.memset(ident[:, :], 0.0))
            chain.link(nc.gpsimd.affine_select(out=ident[:, :], in_=ident[:, :], compare_op=ALU.not_equal,
                                               fill=1.0, base=0, pattern=[[-1, P]], channel_multiplier=1))
            nc.gpsimd.tensor_copy(ident16[:, :], ident[:, :]).then_inc(consts, 1)
            nc.gpsimd.memset(half_neg[:, :], -0.5).then_inc(consts, 1)
            nc.gpsimd.iota(iota[:, :], pattern=[[1, T]], base=0, channel_multiplier=0,
                           allow_small_or_imprecise_dtypes=True).then_inc(consts, 1)
            pool.wait_ge(consts, 3)

            def ffn_rstd(c):
                pool.wait_ge(ln_var, c + 1)
                nc.gpsimd.tensor_tensor(rstd[:, :], var_eps[:, :], half_neg[:, :], ALU.pow).then_inc(ln_rstd, 1)

            def att_rstd_pool(a):
                pool.wait_ge(att_var, a + 1)
                nc.gpsimd.tensor_tensor(rstd_a[:, :], var_eps_a[:, :], half_neg[:, :], ALU.pow).then_inc(att_rstd, 1)

            def att_skip(a, half, i):
                pool.wait_ge(z_ready, a + 1)
                tiles = tiles_of(half, i)
                chain.link(nc.gpsimd.tensor_tensor(zd[:, :, :], za[:, :, :],
                                                   d_row[:, :].unsqueeze(1).broadcast_to([P, CT, C]), ALU.mult))
                nc.gpsimd.tensor_tensor(x[:, tiles, :], x[:, tiles, :], zd[:, :, :], ALU.add).then_inc(xd_added, 1)

            def y_parts(p, i):
                for g in range(2):
                    n = (p * PAIRS + i) * 2 + g
                    pool.wait_ge(y_weighed, 1 + n + 1)
                    hi, lo = (ys[:, part, 4 * g:4 * g + 4, at(i, 1), :] for part in range(2))
                    src = yf[:, g, :, :].unsqueeze(2)
                    chain.link(nc.gpsimd.tensor_copy(hi, src))
                    nc.gpsimd.tensor_tensor(lo, src, hi, ALU.subtract).then_inc(y_split, 1)

            pool.nop().then_inc(y_split, CREDIT)
            pool.wait_ge(amax_ready, 1)
            nc.gpsimd.partition_all_reduce(amax_all[:, 2:3], amax[:, 2:3], P, bass.bass_isa.ReduceOp.max).then_inc(amax_shared, 1)
            with pool.Fori(0, NCH) as i:
                ffn_rstd(i)
            pool.wait_ge(amax_ready, 2)
            nc.gpsimd.partition_all_reduce(amax_all[:, 0:2], amax[:, 0:2], P, bass.bass_isa.ReduceOp.max).then_inc(amax_shared, 1)
            pool.wait_ge(att_in, 6 * 16)
            for p in range(NPH):
                with chain.loop(0, PAIRS, 2) as i:
                    y_parts(p, i)
                if 0 < p < 3:
                    with chain.loop(0, NCH, 1) as i:
                        att_rstd_pool((p - 1) * NCH + i)
                        att_skip((p - 1) * NCH + i, p - 1, i)
                        ffn_rstd((p + 1) * NCH + i)
                elif p == 0:
                    with pool.Fori(0, NCH) as i:
                        ffn_rstd((p + 1) * NCH + i)

        @block.scalar
        def _(act):
            chain = Chain(act, act_chain)

            def xt_copy(c):
                act.wait_ge(xt_ready, c + 1)
                nc.scalar.copy(xt[:, :, :, :], side16).then_inc(xt_copied, 1)

            def zt_copy(a):
                act.wait_ge(zt_ready, a + 1)
                nc.scalar.copy(zt[:, :], side).then_inc(zt_copied, 1)

            def softmax_exp(ph):
                act.wait_ge(sdiff_ready, ph + 1)
                nc.scalar.activation(sexp[:, :, :], sdiff[:, :, :], ACT.Exp, scale=exp_scale[:, :]).then_inc(sexp_ready, 1)

            def turned_copy(p, b, k):
                act.wait_ge(turned, p * HB + b + 1)
                if not (p == 0 and isinstance(b, int) and b < 2):
                    act.wait_ge(gathered, p * HB + b - 1)
                nc.scalar.copy(onehot_t[:, k, :, :].rearrange("p h s -> p (h s)"),
                               ps[:, Y_BANK + k, :].bitcast(FP16)).then_inc(turned_copied, 1)

            def high_copy(p, b, k):
                act.wait_ge(gathered, p * HB + b + 1)
                nc.scalar.copy(xin[:, 0, :, at(b, 1), :],
                               ps[:, 2 * k, :].rearrange("p (e o s) -> p e o s", e=E, o=1)).then_inc(high_copied, 1)

            def gelu(p, i, u):
                n = p * UNITS + i * 4 + u
                act.wait_ge(up_done, n + 1)
                act.wait_ge(h_low, n + 1)
                nc.scalar.activation(hf[:, u % 2, :], ps[:, 2 * (u % 2):2 * (u % 2) + 2, :].rearrange("p a b -> p (a b)"),
                                     ACT.Gelu, scale=gelu_scale[:, :]).then_inc(gelu_done, 1)
                if u in ACT_HIGH:
                    act.wait_ge(gelu_done, CREDIT + n + 1)
                    nc.scalar.activation(hs[:, u, 0, :], hf[:, u % 2, :], ACT.Copy, scale=h_scale[:, :]).then_inc(h_high, 1)

            def y_copy(p, i, k):
                act.wait_ge(down_done, p * E + i * 2 + k + 1)
                nc.scalar.copy(yt[:, :, k, :], ps[:, Y_BANK, :].rearrange("p (b s) -> p b s", b=HB)).then_inc(y_copied, 1)

            act.nop().then_inc(high_copied, CREDIT)
            act.nop().then_inc(gelu_done, CREDIT)
            act.nop().then_inc(y_copied, 1)
            act.wait_ge(gate_in, 16)
            act.wait_ge(scales_ready, 1)
            nc.scalar.activation(gws[:, 0, :], gwf[:, :], ACT.Copy, scale=scale[:, 2:3]).then_inc(gate_high, 1)
            with act.Fori(0, NCH) as i:
                xt_copy(i)
            softmax_exp(0)
            act.wait_ge(att_in, 6 * 16)
            nc.scalar.activation(exp_a[:, :], log_a[:, :], ACT.Exp).then_inc(loga_exp, 1)
            act.wait_ge(scales_ready, 2)
            act.wait_ge(w1_in, 16)
            act.wait_ge(w2_in, 16)
            nc.scalar.activation(w1s[:, 0, :, :], w1f[:, :, :], ACT.Copy, scale=scale[:, 0:1]).then_inc(w_high, 1)
            nc.scalar.activation(w2s[:, 0, :, :, :], w2f[:, :, :, :], ACT.Copy, scale=scale[:, 1:2]).then_inc(w_high, 1)
            for p in range(NPH):
                turned_copy(p, 0, 0)
                turned_copy(p, 1, 1)
                with act.Fori(0, HB // 2 - 1) as i:
                    high_copy(p, 2 * i, 0)
                    turned_copy(p, 2 * i + 2, 0)
                    high_copy(p, 2 * i + 1, 1)
                    turned_copy(p, 2 * i + 3, 1)
                high_copy(p, HB - 2, 0)
                high_copy(p, HB - 1, 1)

                for u in range(3):
                    gelu(p, 0, u)
                with act.Fori(0, PAIRS - 1) as i:
                    gelu(p, i, 3)
                    gelu(p, i + 1, 0)
                    y_copy(p, i, 0)
                    gelu(p, i + 1, 1)
                    gelu(p, i + 1, 2)
                    y_copy(p, i, 1)
                gelu(p, PAIRS - 1, 3)
                y_copy(p, PAIRS - 1, 0)
                y_copy(p, PAIRS - 1, 1)
                if p < NPH - 1:
                    with act.Fori(0, NCH) as i:
                        if p > 0:
                            zt_copy((p - 1) * NCH + i)
                        xt_copy((p + 1) * NCH + i)
                    softmax_exp(p + 1)

        @block.vector
        def _(dve):
            chain = Chain(dve, dve_chain)
            link = chain.link

            def centre(tiles, z, total, ve, ready):
                link(nc.vector.tensor_scalar(z[:, :, :], x[:, tiles, :], 1.0, None, ALU.mult))
                link(nc.vector.tensor_reduce(total[:, :], z[:, :, :], AX.X, ALU.add))
                link(nc.vector.tensor_scalar(total[:, :], total[:, :], 1.0 / C, None, ALU.mult))
                link(nc.vector.tensor_tensor(z[:, :, :], z[:, :, :], total[:, :].unsqueeze(2).broadcast_to([P, CT, C]), ALU.subtract))
                link(nc.vector.tensor_tensor(squares[:, :, :], z[:, :, :], z[:, :, :], ALU.mult))
                link(nc.vector.tensor_reduce(total[:, :], squares[:, :, :], AX.X, ALU.add))
                nc.vector.tensor_scalar(ve[:, :], total[:, :], 1.0 / C, EPS, ALU.mult, ALU.add).then_inc(ready, 1)

            def normalise(z, r):
                return nc.vector.tensor_tensor(z[:, :, :], z[:, :, :], r[:, :].unsqueeze(2).broadcast_to([P, CT, C]), ALU.mult)

            def ffn_norm(c, half, i):
                centre(tiles_of(half, i), zf, mean, var_eps, ln_var)
                dve.wait_ge(ln_rstd, c + 1)
                link(normalise(zf, rstd))
                hi, lo = (xn[:, part, at(i * CT, CT), :] for part in range(2))
                link(nc.vector.tensor_scalar(hi, zf[:, :, :], LN_SCALE, None, ALU.mult))
                nc.vector.scalar_tensor_tensor(lo, zf[:, :, :], LN_SCALE, hi, ALU.mult, ALU.subtract).then_inc(xn_ready, 1)
                dve.wait_ge(xn_ready, c + 1)

            def att_chunk(a, half, i):
                centre(tiles_of(half, i), za, mean_a, var_eps_a, att_var)
                dve.wait_ge(att_rstd, a + 1)
                normalise(za, rstd_a).then_inc(z_ready, 1)
                dve.wait_ge(u_ready, a + 1)
                link(nc.vector.tensor_scalar(bt[:, :], side, b_in[:, :], b_vec[:, :], ALU.add, ALU.mult))
                for b in range(CB):
                    rows = slice(b * T, (b + 1) * T)
                    last = nc.vector.tensor_tensor_scan(hseq[:, rows], decay[:, :], bt[:, rows], 0.0, ALU.mult, ALU.add)
                last.then_inc(hseq_ready, 1)
                dve.wait_ge(v_ready, a + 1)
                dve.wait_ge(xd_added, a + 1)
                xs = x[:, tiles_of(half, i), :]
                nc.vector.tensor_tensor(xs, side.rearrange("p (t c) -> p t c", t=CT), xs, ALU.add).then_inc(v_added, 1)
                dve.wait_ge(v_added, a + 1)

            def softmax_topk(ph):
                dve.wait_ge(scored, (ph + 1) * NCH)
                sc = score.rearrange("p h b e -> p (h b) e")
                link(nc.vector.tensor_reduce(smax[:, :], sc, AX.X, ALU.max))
                nc.vector.tensor_tensor(sdiff[:, :, :], sc, smax[:, :].unsqueeze(2).broadcast_to([P, HT, E]),
                                        ALU.subtract).then_inc(sdiff_ready, 1)
                dve.wait_ge(sexp_ready, ph + 1)
                link(nc.vector.tensor_reduce(ssum[:, :], sexp[:, :, :], AX.X, ALU.add))
                link(nc.vector.reciprocal(srec[:, :], ssum[:, :]))
                nc.vector.tensor_tensor(probs[:, :, :], sexp[:, :, :], srec[:, :].unsqueeze(2).broadcast_to([P, HT, E]),
                                        ALU.mult).then_inc(probs_ready, 1)
                dve.wait_ge(pt_turned, ph + 1)
                link(nc.vector.tensor_copy(ranked[:, 0, :], side[0:RW, 0:T]))
                for r in range(ROUNDS):
                    best = top[:, at(8 * r, 8)]
                    link(nc.vector.max(best, ranked[:, 0, :]))
                    nc.vector.max_index(idx[:, at(8 * r, 8)], best, ranked[:, 0, :])
                    link(nc.vector.match_replace(ranked[:, 0, :], best, ranked[:, 0, :], -1.0))
                nc.vector.tensor_copy(idx2[:, :, :], idx[:, :].unsqueeze(1).broadcast_to([RW, 2, CAP]))
                nc.vector.tensor_scalar(top2[:, :, :], top[:, :].unsqueeze(1).broadcast_to([RW, 2, CAP]), Y_SCALE, None,
                                        ALU.mult).then_inc(topk_ready, 1)
                dve.wait_ge(topk_turned, ph + 1)
                for dst, at0 in ((idx_s, 0), (top_s, RW)):
                    src = side[:, at0:at0 + RW].rearrange("p (b q o) -> p o q b", q=PAIRS, o=2)
                    for par in range(2):
                        rows = slice(par * CAP, (par + 1) * CAP)
                        last = nc.vector.tensor_copy(dst[rows, :, :], src[rows, par, :, :])
                link(last)

            def build(p, b):
                for q in range(PAIRS):
                    last = nc.vector.tensor_scalar(onehot[:, at(b, 1), q, :], iota[:, :].unsqueeze(1),
                                                   idx_s[:, q, at(b, 1)], None, ALU.is_equal)
                last.then_inc(onehot_ready, 1)

            def low_copy(p, b, k):
                dve.wait_ge(gathered, p * HB + b + 1)
                nc.vector.tensor_scalar(xin[:, 1, :, at(b, 1), :],
                                        ps[:, 2 * k + 1, :].rearrange("p (e o s) -> p e o s", e=E, o=1),
                                        1.0, None, ALU.mult).then_inc(low_copied, 1)

            def h_parts(p, i, u):
                n = p * UNITS + i * 4 + u
                if u not in ACT_HIGH:
                    dve.wait_ge(gelu_done, CREDIT + n + 1)
                    link(nc.vector.tensor_scalar(hs[:, u, 0, :], hf[:, u % 2, :], h_scale[:, :], None, ALU.mult))
                else:
                    dve.wait_ge(h_high, (p * PAIRS + i) * len(ACT_HIGH) + ACT_HIGH.index(u) + 1)
                nc.vector.scalar_tensor_tensor(hs[:, u, 1, :], hf[:, u % 2, :], h_scale[:, :], hs[:, u, 0, :],
                                               ALU.mult, ALU.subtract).then_inc(h_low, 1)

            def y_weigh(p, i, g):
                n = (p * PAIRS + i) * 2 + g
                dve.wait_ge(y_turned, n + 1)
                dve.wait_ge(y_split, n + 1)
                nc.vector.tensor_tensor(yf[:, g, :, :], ps[:, TY_BANK, :].rearrange("p (b c) -> p b c", b=4),
                                        top_s[:, at(i, 1), 4 * g:4 * g + 4].rearrange("p o b -> p (o b)").unsqueeze(2).broadcast_to([P, 4, C]),
                                        ALU.mult).then_inc(y_weighed, 1)

            def x_update(p, b, k):
                dve.wait_ge(scattered, p * HB + b + 1)
                xs = x[:, at((p % 2) * HT + b * TH, TH), :]
                nc.vector.scalar_tensor_tensor(xs, ps[:, 2 * k, 0:TH * C].rearrange("p (h c) -> p h c", h=TH),
                                               out_scale[:, :], xs, ALU.mult, ALU.add).then_inc(x_updated, 1)

            dve.nop().then_inc(low_copied, CREDIT)
            dve.nop().then_inc(h_low, CREDIT)
            dve.nop().then_inc(y_weighed, 1)
            dve.nop().then_inc(x_updated, CREDIT)

            def pow2_scale(cols, n):
                dve.wait_ge(amax_shared, n)
                link(nc.vector.tensor_scalar(pow2[:, cols].bitcast(INT32), amax_all[:, cols].bitcast(INT32),
                                             EXP_BITS, None, ALU.bitwise_and))
                link(nc.vector.tensor_scalar(pow2[:, cols], pow2[:, cols], 2.0 ** -100, None, ALU.max))
                link(nc.vector.reciprocal(scale[:, cols], pow2[:, cols]))
                link(nc.vector.tensor_scalar(scale[:, cols], scale[:, cols], W_TOP, None, ALU.mult))

            dve.wait_ge(gate_in, 16)
            nc.vector.tensor_reduce(amax[:, 2:3], gwf[:, :], AX.X, ALU.max, apply_absolute_value=True).then_inc(amax_ready, 1)
            pow2_scale(slice(2, 3), 1)
            nc.vector.tensor_scalar(exp_scale[:, :], pow2[:, 2:3], 1.0 / (W_TOP * LN_SCALE), None, ALU.mult).then_inc(scales_ready, 1)
            dve.wait_ge(gate_high, 1)
            nc.vector.scalar_tensor_tensor(gws[:, 1, :], gwf[:, :], scale[:, 2:3], gws[:, 0, :],
                                           ALU.mult, ALU.subtract).then_inc(gate_split, 1)
            dve.wait_ge(x_in[0], 2 * 16)
            with chain.loop(0, NCH, 8) as i:
                ffn_norm(i, 0, i)
            dve.wait_ge(w1_in, 16)
            nc.vector.tensor_reduce(amax[:, 0:1], w1f[:, :, :], AX.XY, ALU.max, apply_absolute_value=True)
            dve.wait_ge(w2_in, 16)
            nc.vector.tensor_reduce(amax[:, 1:2], w2f[:, :, :, :], AX.XYZ, ALU.max, apply_absolute_value=True).then_inc(amax_ready, 1)
            pow2_scale(slice(0, 2), 2)
            nc.vector.tensor_scalar(h_scale[:, :], scale[:, 0:1], 2.0 ** -6, None, ALU.mult)
            nc.vector.tensor_scalar(out_scale[:, :], pow2[:, 0:1], pow2[:, 1:2],
                                    0.5 * 2.0 ** 6 / (W_TOP * W_TOP * Y_SCALE), ALU.mult, ALU.mult)
            nc.vector.tensor_scalar(gelu_scale[:, :], pow2[:, 0:1], 1.0 / (W_TOP * LN_SCALE), None, ALU.mult).then_inc(scales_ready, 1)
            softmax_topk(0)
            dve.wait_ge(w_high, 2)
            nc.vector.scalar_tensor_tensor(w1s[:, 1, :, :], w1f[:, :, :], scale[:, 0:1], w1s[:, 0, :, :], ALU.mult, ALU.subtract)
            nc.vector.scalar_tensor_tensor(w2s[:, 1, :, :, :].rearrange("p e k c -> p (e k c)"),
                                           w2f[:, :, :, :].rearrange("p e k c -> p (e k c)"), scale[:, 1:2],
                                           w2s[:, 0, :, :, :].rearrange("p e k c -> p (e k c)"),
                                           ALU.mult, ALU.subtract).then_inc(w_split, 1)
            dve.wait_ge(loga_exp, 1)
            nc.vector.memset(decay[:, :], -1.0).then_inc(decay_ready, 1)
            dve.wait_ge(decay_ready, 1)
            link(nc.vector.tensor_scalar(decay[:, :], decay[:, :], exp_a[:, :], None, ALU.mult))
            dve.wait_ge(x_in[1], 16)
            dve.wait_ge(consts, 3)
            for p in range(NPH):
                build(p, 0)
                build(p, 1)
                with dve.Fori(0, HB // 2 - 1) as i:
                    build(p, 2 * i + 2)
                    low_copy(p, 2 * i, 0)
                    build(p, 2 * i + 3)
                    low_copy(p, 2 * i + 1, 1)
                low_copy(p, HB - 2, 0)
                low_copy(p, HB - 1, 1)

                for u in range(4):
                    h_parts(p, 0, u)
                with chain.loop(0, PAIRS - 1, 4 - len(ACT_HIGH)) as i:
                    h_parts(p, i + 1, 0)
                    h_parts(p, i + 1, 1)
                    h_parts(p, i + 1, 2)
                    y_weigh(p, i, 0)
                    y_weigh(p, i, 1)
                    h_parts(p, i + 1, 3)
                y_weigh(p, PAIRS - 1, 0)
                y_weigh(p, PAIRS - 1, 1)

                with dve.Fori(0, HB // 2) as i:
                    x_update(p, 2 * i, 0)
                    x_update(p, 2 * i + 1, 1)
                dve.wait_ge(x_updated, CREDIT + (p + 1) * HB)
                if p < NPH - 1:
                    with chain.loop(0, NCH, 8 if p == 0 else 15) as i:
                        if p > 0:
                            att_chunk((p - 1) * NCH + i, p - 1, i)
                        ffn_norm((p + 1) * NCH + i, (p + 1) % 2, i)
                    softmax_topk(p + 1)

        @block.tensor
        def _(pe):
            def att_turn(a):
                pe.wait_ge(z_ready, a + 1)
                for t in range(CT):
                    last = nc.tensor.transpose(side[:, t * P:(t + 1) * P], za[:, t, :], ident[:, :])
                last.then_inc(zt_ready, 1)

            def att_in_proj(a):
                pe.wait_ge(zt_copied, a + 1)
                nc.tensor.matmul(side, w_in[:, :], zt[:, :], start=True, stop=True).then_inc(u_ready, 1)

            def att_out_proj(a):
                pe.wait_ge(hseq_ready, a + 1)
                for t in range(CT):
                    last = nc.tensor.matmul(side[:, t * P:(t + 1) * P], hseq[:, t * P:(t + 1) * P], c_mat[:, :],
                                            start=True, stop=True)
                last.then_inc(v_ready, 1)

            def xn_turn(c, i):
                pe.wait_ge(xn_ready, c + 1)
                for t in range(CT):
                    for part in range(2):
                        last = nc.tensor.transpose(side16[:, t, part, :], xn[:, part, i * CT + t, :], ident16[:, :])
                last.then_inc(xt_ready, 1)

            def scores(c, i):
                pe.wait_ge(xt_copied, c + 1)
                for t in range(CT):
                    dst = score[:, t % TH, i * CB + t // TH, :]
                    for k, (a, b) in enumerate(((0, 0), (0, 1), (1, 0))):
                        last = nc.tensor.matmul(dst, xt[:, t, a, :], gws[:, b, :], start=(k == 0), stop=(k == 2))
                last.then_inc(scored, 1)

            def turn_probs(ph):
                pe.wait_ge(probs_ready, ph + 1)
                for h in range(TH):
                    last = nc.tensor.transpose(side[0:RW, h * P:(h + 1) * P],
                                               probs[:, h * HB:(h + 1) * HB, :].rearrange("p b e -> p (b e)"), ident[:, :])
                last.then_inc(pt_turned, 1)
                pe.wait_ge(topk_ready, ph + 1)
                for k, m in enumerate((idx2, top2)):
                    last = nc.tensor.transpose(side[:, k * RW:(k + 1) * RW], m[:, :, :].rearrange("r a s -> r (a s)"),
                                               ident[0:RW, 0:RW])
                last.then_inc(topk_turned, 1)

            def turn_onehot(p, b, k):
                pe.wait_ge(onehot_ready, p * HB + b + 1)
                dst = ps[:, Y_BANK + k, :].bitcast(FP16).rearrange("p (h q s) -> p h q s", h=TH, q=PAIRS)
                for h in range(TH):
                    for q in range(PAIRS):
                        last = nc.tensor.transpose(dst[:, h, q, :], onehot[:, b, q, h * P:(h + 1) * P], ident16[:, :])
                last.then_inc(turned, 1)

            def gather(p, b, k):
                pe.wait_ge(turned_copied, p * HB + b + 1)
                pe.wait_ge(high_copied, p * HB + b + 1)
                pe.wait_ge(low_copied, p * HB + b + 1)
                for part in range(2):
                    for h in range(TH):
                        last = nc.tensor.matmul(ps[:, 2 * k + part, :], xn[:, part, b * TH + h, :], onehot_t[:, k, h, :],
                                                start=(h == 0), stop=(h == TH - 1))
                last.then_inc(gathered, 1)

            def up(p, i, u):
                n = p * UNITS + i * 4 + u
                pe.wait_ge(gelu_done, n + 1)
                e = i * 2 + u // 2
                for j in range(2):
                    cols = slice((2 * (u % 2) + j) * P, (2 * (u % 2) + j + 1) * P)
                    for k, (a, b) in enumerate(((0, 0), (0, 1), (1, 0))):
                        last = nc.tensor.matmul(ps[:, 2 * (u % 2) + j, :], w1s[:, a, e, cols],
                                                xin[:, b, e, :, :].rearrange("p b s -> p (b s)"),
                                                start=(k == 0), stop=(k == 2))
                last.then_inc(up_done, 1)

            def down(p, i, u):
                n = p * UNITS + i * 4 + u
                e = i * 2 + u // 2
                pe.wait_ge(h_low, CREDIT + n + 1)
                if u % 2 == 0:
                    pe.wait_ge(y_copied, p * E + e + 1)
                for j in range(2):
                    for k, (a, b) in enumerate(((0, 0), (1, 0), (0, 1))):
                        last = nc.tensor.matmul(ps[:, Y_BANK, :], w2s[:, a, e, 2 * (u % 2) + j, :],
                                                hs[:, u, b, j * SLOTS:(j + 1) * SLOTS],
                                                start=(u % 2 == 0 and j == 0 and k == 0), stop=(u % 2 == 1 and j == 1 and k == 2))
                if u % 2 == 1:
                    last.then_inc(down_done, 1)

            def turn_y(p, i, g):
                n = (p * PAIRS + i) * 2 + g
                pe.wait_ge(y_copied, 1 + p * E + i * 2 + 2)
                pe.wait_ge(y_weighed, n + 1)
                for b in range(4):
                    last = nc.tensor.transpose(ps[:, TY_BANK, b * P:(b + 1) * P], yt[:, 4 * g + b, :, :].rearrange("p a s -> p (a s)"), ident[:, :])
                last.then_inc(y_turned, 1)

            def scatter(p, b, k):
                pe.wait_ge(x_updated, p * HB + b + 1)
                for h in range(TH):
                    for q in range(PAIRS):
                        for part in range(2):
                            last = nc.tensor.matmul(ps[:, 2 * k, h * C:(h + 1) * C], onehot[:, b, q, h * P:(h + 1) * P],
                                                    ys[:, part, b, q, :], start=(q == 0 and part == 0),
                                                    stop=(q == PAIRS - 1 and part == 1))
                last.then_inc(scattered, 1)

            pe.wait_ge(consts, 3)
            pe.wait_ge(gate_split, 1)
            with pe.Fori(0, NCH) as i:
                xn_turn(i, i)
                scores(i, i)
            turn_probs(0)
            for p in range(NPH):
                turn_onehot(p, 0, 0)
                with pe.Fori(0, HB // 2 - 1) as i:
                    turn_onehot(p, 2 * i + 1, 1)
                    gather(p, 2 * i, 0)
                    turn_onehot(p, 2 * i + 2, 0)
                    gather(p, 2 * i + 1, 1)
                turn_onehot(p, HB - 1, 1)
                gather(p, HB - 2, 0)
                gather(p, HB - 1, 1)

                pe.wait_ge(high_copied, CREDIT + (p + 1) * HB)
                pe.wait_ge(low_copied, CREDIT + (p + 1) * HB)
                pe.wait_ge(w_split, 1)
                for u in range(4):
                    up(p, 0, u)
                down(p, 0, 0)
                with pe.Fori(0, PAIRS - 1) as i:
                    for u in range(1, 4):
                        up(p, i + 1, u - 1)
                        down(p, i, u)
                    up(p, i + 1, 3)
                    turn_y(p, i, 0)
                    down(p, i + 1, 0)
                    turn_y(p, i, 1)
                for u in range(1, 4):
                    down(p, PAIRS - 1, u)
                turn_y(p, PAIRS - 1, 0)
                turn_y(p, PAIRS - 1, 1)

                pe.wait_ge(y_split, CREDIT + (p + 1) * PAIRS * 2)
                with pe.Fori(0, HB // 2) as i:
                    scatter(p, 2 * i, 0)
                    scatter(p, 2 * i + 1, 1)
                if p < NPH - 1:
                    if p == 1:
                        pe.wait_ge(att_in, 6 * 16)
                    with pe.Fori(0, NCH) as i:
                        if p > 0:
                            a = (p - 1) * NCH + i
                            att_turn(a)
                            att_in_proj(a)
                            att_out_proj(a)
                            pe.wait_ge(v_added, a + 1)
                        xn_turn((p + 1) * NCH + i, i)
                        scores((p + 1) * NCH + i, i)
                    turn_probs(p + 1)


ACT_HIGH = (0, 2)


_INS = ['L0_attn_x', 'L0_attn_W_in', 'L0_attn_b_in', 'L0_attn_log_A', 'L0_attn_B_vec', 'L0_attn_C', 'L0_attn_D',
        'L0_ffn_gate_w', 'L0_ffn_w1', 'L0_ffn_w2']


def kernel(**inputs):
    import numpy as _np
    import concourse.bacc as _bacc
    from concourse import mybir as _mybir
    from concourse.bass_utils import run_bass_kernel_spmd as _run

    nc = _bacc.Bacc("TRN2", target_bir_lowering=False, num_devices=1)
    arrays, args = {}, []
    for name in _INS:
        a = _np.ascontiguousarray(inputs[name])
        arrays[f"in_{name}_dram"] = a
        args.append(nc.dram_tensor(f"in_{name}_dram", a.shape, _mybir.dt.from_np(a.dtype), kind="ExternalInput").ap())
    shape = inputs['L0_attn_x'].shape
    out = nc.dram_tensor("out_dram", shape, _mybir.dt.float32, kind="ExternalOutput").ap()
    macaron_kernel(nc, *args, out)
    r = _run(nc, [arrays], core_ids=[0])
    return r.results[0]["out_dram"]
```

```python
import numpy as np
from contextlib import ExitStack, contextmanager

import concourse.bass as bass
from concourse import mybir

FP32 = mybir.dt.float32
FP16 = mybir.dt.float16
INT32 = mybir.dt.int32
UINT32 = mybir.dt.uint32
ALU = mybir.AluOpType
ACT = mybir.ActivationFunctionType
AX = mybir.AxisListType
RED = bass.bass_isa.ReduceOp


class Chain:

    def __init__(self, eng, sem):
        self.eng, self.sem = eng, sem
        self.base, self.local, self.offset = 0, 0, 0

    def link(self, instruction):
        instruction.then_inc(self.sem, 1)
        self.local += 1
        self.eng.wait_ge(self.sem, self.offset + self.base + self.local)

    @contextmanager
    def loop(self, start, end, links):
        self.base, self.local = self.base + self.local, 0
        with self.eng.Fori(start, end) as i:
            self.offset = i * links
            self.base -= start * links
            yield i
            assert self.local == links, (self.local, links)
            self.base += start * links
        self.base, self.local, self.offset = self.base + (end - start) * links, 0, 0


def macaron_kernel(nc, x_d, w_in_d, b_in_d, log_a_d, b_vec_d, c_d, d_d, gate_d, w1_d, w2_d, out_d):
    B, T, C = x_d.shape
    E, _, H = w1_d.shape
    P = 128
    TH = T // P
    CAP = 2 * T // E
    HB = B // 2
    NPH = 4
    NCH = 4
    CB = HB // NCH
    CT = CB * TH
    HT = HB * TH
    PAIRS = E // 2
    HC = H // P
    UNITS = 2 * PAIRS * 2
    SLOTS = HB * CAP
    ROUNDS = CAP // 8
    assert C == P and SLOTS == 512 and 2 * CAP == P and HC == 4 and NCH == PAIRS
    EPS = 1e-5
    LN_SCALE = 2.0 ** 10
    GATE_TOP = 2.0 ** 13
    W_TOP = 2.0 ** 15
    H_SCALE = 2.0 ** -4
    Y_SCALE = 2.0 ** -15
    EXP_BITS = 0x7F800000
    act_high = [(0, 2), (0, 1, 2, 3), (0, 1, 2, 3), (0, 2)]
    highs = [0, 8, 24, 40]

    ctx = ExitStack()
    with ctx:
        def sb(name, shape, dt=FP32):
            return ctx.enter_context(nc.sbuf_tensor(name, shape, dt))

        def sem(name):
            return ctx.enter_context(nc.semaphore(name))

        x = sb("x", [P, B * TH, C])
        w1f = sb("w1f", [P, E, H])
        w2f = sb("w2f", [P, E, HC, C])
        w1s = sb("w1s", [P, 2, E, H], FP16)
        w2s = sb("w2s", [P, 2, E, HC, C], FP16)
        gwf = sb("gwf", [P, E])
        gws = sb("gws", [P, 2, E], FP16)
        w_in = sb("w_in", [P, P])
        c_mat = sb("c_mat", [P, P])
        d_row = sb("d_row", [P, C])
        b_in = sb("b_in", [P, 1])
        b_vec = sb("b_vec", [P, 1])
        log_a = sb("log_a", [P, 1])
        exp_a = sb("exp_a", [P, 1])
        decay = sb("decay", [P, T])
        ident = sb("ident", [P, P])
        ident16 = sb("ident16", [P, P], FP16)
        iota = sb("iota", [P, T], FP16)
        half_neg = sb("half_neg", [P, CT])
        amax = sb("amax", [P, 4])
        amax_all = sb("amax_all", [P, 4])
        pow2 = sb("pow2", [P, 4])
        scale = sb("scale", [P, 4])
        gelu_scale = sb("gelu_scale", [P, 1])
        h_scale = sb("h_scale", [P, 1])
        exp_scale = sb("exp_scale", [P, 1])
        out_scale = sb("out_scale", [P, 1])

        stats = sb("stats", [P, NCH, CT, 6])
        mv = sb("mv", [P, NCH, CT, 2])
        var_eps = sb("var_eps", [P, NCH, CT])
        rstd = sb("rstd", [P, NCH, CT])
        stats_a = sb("stats_a", [P, CT, 6])
        mv_a = sb("mv_a", [P, CT, 2])
        var_eps_a = sb("var_eps_a", [P, CT])
        rstd_a = sb("rstd_a", [P, CT])
        zf = sb("zf", [P, CT, C])
        xn = sb("xn", [P, 2, HT, C], FP16)
        xt = sb("xt", [P, CT, 2, P], FP16)
        za = sb("za", [P, CT, C])
        zd = sb("zd", [P, CT, C])
        zt = sb("zt", [P, CT * P])
        bt = sb("bt", [P, CT * P])
        hseq = sb("hseq", [P, CT * P])

        smax = sb("smax", [P, HT])
        sdiff = sb("sdiff", [P, HT, E])
        sexp = sb("sexp", [P, HT, E])
        ssum = sb("ssum", [P, HT])
        srec = sb("srec", [P, HT])
        probs = sb("probs", [P, HT, E])
        RW = HB * E
        ranked = sb("ranked", [RW, T])
        top = sb("top", [RW, CAP])
        idx = sb("idx", [RW, CAP], UINT32)
        top2 = sb("top2", [RW, 2, CAP])
        idx2 = sb("idx2", [RW, 2, CAP])
        idx_s = sb("idx_s", [P, PAIRS, HB])
        top_s = sb("top_s", [P, PAIRS, HB])

        onehot = sb("onehot", [P, HB, PAIRS, T], FP16)
        onehot_t = sb("onehot_t", [P, 2, TH, PAIRS * P], FP16)
        xin = sb("xin", [P, 2, E, HB, CAP], FP16)
        hf = sb("hf", [P, 2, 2 * SLOTS])
        hs = sb("hs", [P, 4, 2, 2 * SLOTS], FP16)
        yt = sb("yt", [P, HB, 2, CAP])
        yf = sb("yf", [P, 2, 4, C])
        ys = sb("ys", [P, 2, HB, PAIRS, C], FP16)

        ps = ctx.enter_context(nc.psum_tensor("ps", [P, 8, 512], FP32))
        Y_BANK, TY_BANK, SIDE_BANK, SCORE_BANK = 4, 5, 6, 7
        side = ps[:, SIDE_BANK, :]
        xt_bank = ps[:, TY_BANK, :].bitcast(FP16).rearrange("p (t s c) -> p t s c", t=CT, s=2)
        score = ps[:, SCORE_BANK, 0:HT * E].rearrange("p (h b e) -> p h b e", h=TH, e=E)

        x_in = [sem(f"x_in{h}") for h in range(2)]
        gate_in, w1_in, w2_in, att_in = sem("gate_in"), sem("w1_in"), sem("w2_in"), sem("att_in")
        consts = sem("consts")
        gate_max, gate_shared, gate_scaled = sem("gate_max"), sem("gate_shared"), sem("gate_scaled")
        w_squares, w_shared, w_scaled = sem("w_squares"), sem("w_shared"), sem("w_scaled")
        w_high, w1_split, w2_split = sem("w_high"), sem("w1_split"), sem("w2_split")
        gate_high, gate_split = sem("gate_high"), sem("gate_split")
        loga_exp, decay_ready = sem("loga_exp"), sem("decay_ready")
        dve_chain, act_chain, pool_chain = sem("dve_chain"), sem("act_chain"), sem("pool_chain")
        ln_var, ln_rstd, xn_ready = sem("ln_var"), sem("ln_rstd"), sem("xn_ready")
        xt_ready, xt_copied, scored = sem("xt_ready"), sem("xt_copied"), sem("scored")
        sdiff_ready, sexp_ready, probs_ready = sem("sdiff_ready"), sem("sexp_ready"), sem("probs_ready")
        pt_turned, topk_ready, topk_turned = sem("pt_turned"), sem("topk_ready"), sem("topk_turned")
        onehot_ready, turned, turned_copied = sem("onehot_ready"), sem("turned"), sem("turned_copied")
        gathered, high_copied, low_copied = sem("gathered"), sem("high_copied"), sem("low_copied")
        up_done, gelu_done, h_high, h_low = sem("up_done"), sem("gelu_done"), sem("h_high"), sem("h_low")
        down_done, y_copied = sem("down_done"), sem("y_copied")
        y_turned, y_weighed, y_high, y_split = sem("y_turned"), sem("y_weighed"), sem("y_high"), sem("y_split")
        scattered, x_updated = sem("scattered"), sem("x_updated")
        att_var, att_rstd, z_ready, xd_added = sem("att_var"), sem("att_rstd"), sem("z_ready"), sem("xd_added")
        zt_ready, zt_copied, u_ready = sem("zt_ready"), sem("zt_copied"), sem("u_ready")
        hseq_ready, v_ready, v_added = sem("hseq_ready"), sem("v_ready"), sem("v_added")
        out_sent = sem("out_sent")

        CREDIT = 2

        def tiles_of(half, i):
            return bass.ds(half * HT + i * CT, CT) if not isinstance(i, int) else slice(half * HT + i * CT, half * HT + (i + 1) * CT)

        def at(i, n):
            return bass.ds(i, n) if not isinstance(i, int) else slice(i, i + n)

        block = ctx.enter_context(nc.Block())

        @block.sync
        def _(sp):
            xv = x_d.rearrange("b (h p) c -> p (b h) c", p=P)
            ov = out_d.rearrange("b (h p) c -> p (b h) c", p=P)
            q = HT // 2
            for k in range(2):
                sp.dma_start(x[:, k * q:(k + 1) * q, :], xv[:, k * q:(k + 1) * q, :]).then_inc(x_in[0], 16)
            sp.dma_start(gwf[:, :], gate_d).then_inc(gate_in, 16)
            sp.dma_start(w1f[:, :, :], w1_d.rearrange("e c h -> c e h")).then_inc(w1_in, 16)
            sp.dma_start(w2f[:, :, :, :], w2_d.rearrange("e (k p) c -> p e k c", p=P)).then_inc(w2_in, 16)
            sp.dma_start(x[:, HT:2 * HT, :], xv[:, HT:2 * HT, :]).then_inc(x_in[1], 16)
            sp.dma_start(w_in[:, :], w_in_d).then_inc(att_in, 16)
            sp.dma_start(c_mat[:, :], c_d).then_inc(att_in, 16)
            sp.dma_start(d_row[:, :], d_d.rearrange("(a c) -> a c", a=1).broadcast_to([P, C])).then_inc(att_in, 16)
            for dst, src in ((b_in, b_in_d), (b_vec, b_vec_d), (log_a, log_a_d)):
                sp.dma_start(dst[:, :], src.rearrange("(c a) -> c a", a=1)).then_inc(att_in, 16)
            for half in range(2):
                for k in range(2):
                    lo = half * HT + k * q
                    sp.wait_ge(x_updated, CREDIT + (2 + half) * HB + (k + 1) * HB // 2)
                    sp.dma_start(ov[:, lo:lo + q, :], x[:, lo:lo + q, :]).then_inc(out_sent, 16)
            sp.wait_ge(out_sent, 4 * 16)

        @block.gpsimd
        def _(pool):
            chain = Chain(pool, pool_chain)
            chain.link(nc.gpsimd.memset(ident[:, :], 0.0))
            chain.link(nc.gpsimd.affine_select(out=ident[:, :], in_=ident[:, :], compare_op=ALU.not_equal,
                                               fill=1.0, base=0, pattern=[[-1, P]], channel_multiplier=1))
            nc.gpsimd.tensor_copy(ident16[:, :], ident[:, :]).then_inc(consts, 1)
            nc.gpsimd.memset(half_neg[:, :], -0.5).then_inc(consts, 1)
            nc.gpsimd.iota(iota[:, :], pattern=[[1, T]], base=0, channel_multiplier=0,
                           allow_small_or_imprecise_dtypes=True).then_inc(consts, 1)
            pool.wait_ge(consts, 3)

            def ffn_rstd(c, k=0):
                pool.wait_ge(ln_var, c + 1)
                nc.gpsimd.tensor_tensor(rstd[:, k, :], var_eps[:, k, :], half_neg[:, :], ALU.pow).then_inc(ln_rstd, 1)

            def att_rstd_pool(a):
                pool.wait_ge(att_var, a + 1)
                nc.gpsimd.tensor_tensor(rstd_a[:, :], var_eps_a[:, :], half_neg[:, :], ALU.pow).then_inc(att_rstd, 1)

            def att_skip(a, half, i):
                pool.wait_ge(z_ready, a + 1)
                if not (isinstance(a, int) and a == 0):
                    pool.wait_ge(xd_added, a)
                tiles = tiles_of(half, i)
                chain.link(nc.gpsimd.tensor_tensor(zd[:, :, :], za[:, :, :],
                                                   d_row[:, :].unsqueeze(1).broadcast_to([P, CT, C]), ALU.mult))
                nc.gpsimd.tensor_tensor(x[:, tiles, :], x[:, tiles, :], zd[:, :, :], ALU.add).then_inc(xd_added, 1)

            def y_low(p, i):
                for g in range(2):
                    pool.wait_ge(y_high, (p * PAIRS + i) * 2 + g + 1)
                    hi, lo = (ys[:, part, 4 * g:4 * g + 4, at(i, 1), :] for part in range(2))
                    nc.gpsimd.tensor_tensor(lo, yf[:, g, :, :].unsqueeze(2), hi, ALU.subtract).then_inc(y_split, 1)

            pool.nop().then_inc(y_split, CREDIT)
            pool.wait_ge(gate_max, 1)
            nc.gpsimd.partition_all_reduce(amax_all[:, 2:3], amax[:, 2:3], P, RED.max).then_inc(gate_shared, 1)
            for i in range(NCH):
                ffn_rstd(i, i)
            pool.wait_ge(w_squares, 2)
            nc.gpsimd.partition_all_reduce(amax_all[:, 0:2], amax[:, 0:2], P, RED.add).then_inc(w_shared, 1)
            pool.wait_ge(w_high, 2)
            nc.gpsimd.tensor_tensor(w2s[:, 1, :, :, :], w2f[:, :, :, :], w2s[:, 0, :, :, :], ALU.subtract).then_inc(w2_split, 1)
            for p in range(NPH):
                half, nxt = p - 1, (p + 1) * NCH
                with_att, with_ffn = p in (1, 2), p < NPH - 1
                if with_att:
                    att_rstd_pool(half * NCH)
                    att_skip(half * NCH, half, 0)
                with pool.Fori(0, PAIRS - 1) if not with_att else chain.loop(0, PAIRS - 1, 1) as i:
                    if with_att:
                        att_rstd_pool(half * NCH + i + 1)
                    if with_ffn:
                        ffn_rstd(nxt + i)
                    if with_att:
                        att_skip(half * NCH + i + 1, half, i + 1)
                    y_low(p, i)
                if with_ffn:
                    ffn_rstd(nxt + NCH - 1)
                y_low(p, PAIRS - 1)

        @block.scalar
        def _(act):
            chain = Chain(act, act_chain)

            def xt_copy(c):
                act.wait_ge(xt_ready, c + 1)
                nc.scalar.copy(xt[:, :, :, :], xt_bank).then_inc(xt_copied, 1)

            def zt_copy(a):
                act.wait_ge(zt_ready, a + 1)
                nc.scalar.copy(zt[:, :], side).then_inc(zt_copied, 1)

            def softmax_exp(ph):
                act.wait_ge(sdiff_ready, ph + 1)
                nc.scalar.activation(sexp[:, :, :], sdiff[:, :, :], ACT.Exp, scale=exp_scale[:, :]).then_inc(sexp_ready, 1)

            def turned_copy(p, b, k):
                act.wait_ge(turned, p * HB + b + 1)
                if not (p == 0 and isinstance(b, int) and b < 2):
                    act.wait_ge(gathered, p * HB + b - 1)
                nc.scalar.copy(onehot_t[:, k, :, :].rearrange("p h s -> p (h s)"),
                               ps[:, Y_BANK + k, :].bitcast(FP16)).then_inc(turned_copied, 1)

            def high_copy(p, b, k):
                act.wait_ge(gathered, p * HB + b + 1)
                nc.scalar.copy(xin[:, 0, :, at(b, 1), :],
                               ps[:, 2 * k, :].rearrange("p (e o s) -> p e o s", e=E, o=1)).then_inc(high_copied, 1)

            def gelu(p, i, u):
                n = p * UNITS + i * 4 + u
                act.wait_ge(up_done, n + 1)
                act.wait_ge(h_low, n + 1)
                nc.scalar.activation(hf[:, u % 2, :], ps[:, 2 * (u % 2):2 * (u % 2) + 2, :].rearrange("p a b -> p (a b)"),
                                     ACT.Gelu, scale=gelu_scale[:, :]).then_inc(gelu_done, 1)
                if u in act_high[p]:
                    act.wait_ge(gelu_done, CREDIT + n + 1)
                    nc.scalar.activation(hs[:, u, 0, :], hf[:, u % 2, :], ACT.Copy, scale=h_scale[:, :]).then_inc(h_high, 1)

            def y_high_copy(p, i):
                for g in range(2):
                    act.wait_ge(y_weighed, 1 + (p * PAIRS + i) * 2 + g + 1)
                    nc.scalar.copy(ys[:, 0, 4 * g:4 * g + 4, at(i, 1), :], yf[:, g, :, :].unsqueeze(2)).then_inc(y_high, 1)

            def y_copy(p, i, k):
                act.wait_ge(down_done, p * E + i * 2 + k + 1)
                nc.scalar.copy(yt[:, :, k, :], ps[:, Y_BANK, :].rearrange("p (b s) -> p b s", b=HB)).then_inc(y_copied, 1)

            act.nop().then_inc(high_copied, CREDIT)
            act.nop().then_inc(gelu_done, CREDIT)
            act.nop().then_inc(y_copied, 1)
            act.wait_ge(gate_scaled, 1)
            nc.scalar.activation(gws[:, 0, :], gwf[:, :], ACT.Copy, scale=scale[:, 2:3]).then_inc(gate_high, 1)
            junk = hs[:, :, :, :].rearrange("p u a s -> p (u a s)")[:, 0:E * H]
            act.wait_ge(w1_in, 16)
            nc.scalar.activation(junk, w1f[:, :, :].rearrange("p e h -> p (e h)"), ACT.Square,
                                 accum_out=amax[:, 0:1]).then_inc(w_squares, 1)
            for i in range(NCH):
                xt_copy(i)
            softmax_exp(0)
            act.wait_ge(w2_in, 16)
            act.wait_ge(w_squares, 1)
            nc.scalar.activation(junk, w2f[:, :, :, :].rearrange("p e k c -> p (e k c)"), ACT.Square,
                                 accum_out=amax[:, 1:2]).then_inc(w_squares, 1)
            act.wait_ge(w_scaled, 1)
            nc.scalar.activation(w1s[:, 0, :, :], w1f[:, :, :], ACT.Copy, scale=scale[:, 0:1]).then_inc(w_high, 1)
            act.wait_ge(att_in, 6 * 16)
            nc.scalar.activation(exp_a[:, :], log_a[:, :], ACT.Exp).then_inc(loga_exp, 1)
            chain.link(nc.scalar.activation(w2f[:, :, :, :], w2f[:, :, :, :], ACT.Copy, scale=scale[:, 1:2]))
            nc.scalar.copy(w2s[:, 0, :, :, :], w2f[:, :, :, :]).then_inc(w_high, 1)
            for p in range(NPH):
                turned_copy(p, 0, 0)
                turned_copy(p, 1, 1)
                with act.Fori(0, HB // 2 - 1) as i:
                    high_copy(p, 2 * i, 0)
                    turned_copy(p, 2 * i + 2, 0)
                    high_copy(p, 2 * i + 1, 1)
                    turned_copy(p, 2 * i + 3, 1)
                high_copy(p, HB - 2, 0)
                high_copy(p, HB - 1, 1)

                att, nxt = (p - 1) * NCH, (p + 1) * NCH
                with_att, with_ffn = p in (1, 2), p < NPH - 1
                gelu(p, 0, 0)
                gelu(p, 0, 1)
                if with_att:
                    zt_copy(att)
                gelu(p, 0, 2)
                gelu(p, 0, 3)
                with act.Fori(0, PAIRS - 1) as i:
                    gelu(p, i + 1, 0)
                    y_copy(p, i, 0)
                    gelu(p, i + 1, 1)
                    gelu(p, i + 1, 2)
                    if with_att:
                        zt_copy(att + i + 1)
                    y_copy(p, i, 1)
                    if with_ffn:
                        xt_copy(nxt + i)
                    gelu(p, i + 1, 3)
                    y_high_copy(p, i)
                y_copy(p, PAIRS - 1, 0)
                y_copy(p, PAIRS - 1, 1)
                if with_ffn:
                    xt_copy(nxt + NCH - 1)
                y_high_copy(p, PAIRS - 1)
                if with_ffn:
                    softmax_exp(p + 1)

        @block.vector
        def _(dve):
            chain = Chain(dve, dve_chain)
            link = chain.link

            def statistics(half, i, st):
                for t in range(CT):
                    last = nc.vector.bn_stats(st[:, t, :], x[:, half * HT + i * CT + t, :])
                link(last)

            def variance(st, m, ve, ready, added=None):
                for t in range(CT):
                    last = nc.vector.bn_aggr(m[:, t, :], st[:, t, :])
                link(last)
                if added is not None:
                    dve.wait_ge(v_added, added + 1)
                nc.vector.tensor_scalar(ve, m[:, :, 1], EPS, None, ALU.add).then_inc(ready, 1)

            def normalise(half, i, m, r, z):
                for t in range(CT):
                    last = nc.vector.tensor_scalar(z[:, t, :], x[:, half * HT + i * CT + t, :], m[:, t, 0:1],
                                                   r[:, t:t + 1], ALU.subtract, ALU.mult)
                return last

            def ffn_stats(half, i, k=0):
                statistics(half, i, stats[:, k])

            def ffn_var(k=0):
                variance(stats[:, k], mv[:, k], var_eps[:, k, :], ln_var)

            def ffn_norm(c, half, i, k=0):
                dve.wait_ge(ln_rstd, c + 1)
                link(normalise(half, i, mv[:, k], rstd[:, k, :], zf))
                hi, lo = (xn[:, part, at(i * CT, CT), :] for part in range(2))
                link(nc.vector.tensor_scalar(hi, zf[:, :, :], LN_SCALE, None, ALU.mult))
                nc.vector.scalar_tensor_tensor(lo, zf[:, :, :], LN_SCALE, hi, ALU.mult, ALU.subtract).then_inc(xn_ready, 1)
                dve.wait_ge(xn_ready, c + 1)

            def att_stats(half, i):
                statistics(half, i, stats_a)

            def att_variance(added=None):
                variance(stats_a, mv_a, var_eps_a[:, :], att_var, added)

            def att_norm(a, half, i):
                dve.wait_ge(att_rstd, a + 1)
                normalise(half, i, mv_a, rstd_a, za).then_inc(z_ready, 1)

            def att_scan(a):
                dve.wait_ge(u_ready, a + 1)
                link(nc.vector.tensor_scalar(bt[:, :], side, b_in[:, :], b_vec[:, :], ALU.add, ALU.mult))
                for b in range(CB):
                    rows = slice(b * T, (b + 1) * T)
                    last = nc.vector.tensor_tensor_scan(hseq[:, rows], decay[:, :], bt[:, rows], 0.0, ALU.mult, ALU.add)
                last.then_inc(hseq_ready, 1)

            def att_add(a, half, i):
                dve.wait_ge(v_ready, a + 1)
                dve.wait_ge(xd_added, a + 1)
                xs = x[:, tiles_of(half, i), :]
                nc.vector.tensor_tensor(xs, side.rearrange("p (t c) -> p t c", t=CT), xs, ALU.add).then_inc(v_added, 1)

            def softmax_topk(ph, update=lambda b: None):
                dve.wait_ge(scored, (ph + 1) * NCH)
                sc = score.rearrange("p h b e -> p (h b) e")
                link(nc.vector.tensor_reduce(smax[:, :], sc, AX.X, ALU.max))
                nc.vector.tensor_tensor(sdiff[:, :, :], sc, smax[:, :].unsqueeze(2).broadcast_to([P, HT, E]),
                                        ALU.subtract).then_inc(sdiff_ready, 1)
                update(0)
                update(1)
                dve.wait_ge(sexp_ready, ph + 1)
                link(nc.vector.tensor_reduce(ssum[:, :], sexp[:, :, :], AX.X, ALU.add))
                link(nc.vector.reciprocal(srec[:, :], ssum[:, :]))
                nc.vector.tensor_tensor(probs[:, :, :], sexp[:, :, :], srec[:, :].unsqueeze(2).broadcast_to([P, HT, E]),
                                        ALU.mult).then_inc(probs_ready, 1)
                update(2)
                update(3)
                dve.wait_ge(pt_turned, ph + 1)
                link(nc.vector.tensor_copy(ranked[:, :], side[0:RW, 0:T]))
                for r in range(ROUNDS):
                    best = top[:, 8 * r:8 * r + 8]
                    link(nc.vector.max(best, ranked[:, :]))
                    nc.vector.max_index(idx[:, 8 * r:8 * r + 8], best, ranked[:, :])
                    if 1 <= r <= 4:
                        update(3 + r)
                    link(nc.vector.match_replace(ranked[:, :], best, ranked[:, :], -1.0))
                nc.vector.tensor_copy(idx2[:, :, :], idx[:, :].unsqueeze(1).broadcast_to([RW, 2, CAP]))
                nc.vector.tensor_scalar(top2[:, :, :], top[:, :].unsqueeze(1).broadcast_to([RW, 2, CAP]), Y_SCALE, None,
                                        ALU.mult).then_inc(topk_ready, 1)
                dve.wait_ge(topk_turned, ph + 1)
                for dst, at0 in ((idx_s, 0), (top_s, RW)):
                    src = side[:, at0:at0 + RW].rearrange("p (b q o) -> p o q b", q=PAIRS, o=2)
                    for par in range(2):
                        rows = slice(par * CAP, (par + 1) * CAP)
                        last = nc.vector.tensor_copy(dst[rows, :, :], src[rows, par, :, :])
                link(last)

            def build(p, b):
                for q in range(PAIRS):
                    last = nc.vector.tensor_scalar(onehot[:, at(b, 1), q, :], iota[:, :].unsqueeze(1),
                                                   idx_s[:, q, at(b, 1)], None, ALU.is_equal)
                last.then_inc(onehot_ready, 1)

            def low_copy(p, b, k):
                dve.wait_ge(gathered, p * HB + b + 1)
                nc.vector.tensor_scalar(xin[:, 1, :, at(b, 1), :],
                                        ps[:, 2 * k + 1, :].rearrange("p (e o s) -> p e o s", e=E, o=1),
                                        1.0, None, ALU.mult).then_inc(low_copied, 1)

            def h_parts(p, i, u):
                n = p * UNITS + i * 4 + u
                if u not in act_high[p]:
                    dve.wait_ge(gelu_done, CREDIT + n + 1)
                    link(nc.vector.tensor_scalar(hs[:, u, 0, :], hf[:, u % 2, :], h_scale[:, :], None, ALU.mult))
                else:
                    dve.wait_ge(h_high, highs[p] + i * len(act_high[p]) + act_high[p].index(u) + 1)
                nc.vector.scalar_tensor_tensor(hs[:, u, 1, :], hf[:, u % 2, :], h_scale[:, :], hs[:, u, 0, :],
                                               ALU.mult, ALU.subtract).then_inc(h_low, 1)

            def y_weigh(p, i, g):
                n = (p * PAIRS + i) * 2 + g
                dve.wait_ge(y_turned, n + 1)
                dve.wait_ge(y_split, n + 1)
                nc.vector.tensor_tensor(yf[:, g, :, :], ps[:, TY_BANK, :].rearrange("p (b c) -> p b c", b=4),
                                        top_s[:, at(i, 1), 4 * g:4 * g + 4].rearrange("p o b -> p (o b)").unsqueeze(2).broadcast_to([P, 4, C]),
                                        ALU.mult).then_inc(y_weighed, 1)

            def x_update(p, b, k):
                dve.wait_ge(scattered, p * HB + b + 1)
                xs = x[:, at((p % 2) * HT + b * TH, TH), :]
                nc.vector.scalar_tensor_tensor(xs, ps[:, 2 * k, 0:TH * C].rearrange("p (h c) -> p h c", h=TH),
                                               out_scale[:, :], xs, ALU.mult, ALU.add).then_inc(x_updated, 1)

            dve.nop().then_inc(low_copied, CREDIT)
            dve.nop().then_inc(h_low, CREDIT)
            dve.nop().then_inc(y_weighed, 1)
            dve.nop().then_inc(x_updated, CREDIT)

            def pow2_scale(cols):
                link(nc.vector.tensor_scalar(pow2[:, cols].bitcast(INT32), amax_all[:, cols].bitcast(INT32),
                                             EXP_BITS, None, ALU.bitwise_and))
                link(nc.vector.tensor_scalar(pow2[:, cols], pow2[:, cols], 2.0 ** -60, None, ALU.max))
                link(nc.vector.reciprocal(scale[:, cols], pow2[:, cols]))
                link(nc.vector.tensor_scalar(scale[:, cols], scale[:, cols], GATE_TOP, None, ALU.mult))

            dve.wait_ge(gate_in, 16)
            nc.vector.tensor_reduce(amax[:, 2:3], gwf[:, :], AX.X, ALU.max, apply_absolute_value=True).then_inc(gate_max, 1)
            dve.wait_ge(gate_shared, 1)
            pow2_scale(slice(2, 3))
            nc.vector.tensor_scalar(exp_scale[:, :], pow2[:, 2:3], 1.0 / (GATE_TOP * LN_SCALE), None, ALU.mult).then_inc(gate_scaled, 1)
            for i in range(NCH):
                ffn_stats(0, i, i)
                ffn_var(i)
            dve.wait_ge(gate_high, 1)
            nc.vector.scalar_tensor_tensor(gws[:, 1, :], gwf[:, :], scale[:, 2:3], gws[:, 0, :],
                                           ALU.mult, ALU.subtract).then_inc(gate_split, 1)
            for i in range(NCH):
                ffn_norm(i, 0, i, i)
            def weight_scales(b):
                if b != 4:
                    return
                dve.wait_ge(w_shared, 1)
                link(nc.vector.tensor_scalar(amax_all[:, 0:2], amax_all[:, 0:2], 2.0 ** -100, 2.0 ** 100, ALU.max, ALU.min))
                link(nc.vector.tensor_scalar(pow2[:, 0:2].bitcast(INT32), amax_all[:, 0:2].bitcast(INT32), 1, EXP_BITS,
                                             ALU.logical_shift_right, ALU.bitwise_and))
                link(nc.vector.tensor_scalar(pow2[:, 0:2], pow2[:, 0:2], 2.0 ** 64, None, ALU.mult))
                link(nc.vector.reciprocal(scale[:, 0:2], pow2[:, 0:2]))
                link(nc.vector.tensor_scalar(scale[:, 0:2], scale[:, 0:2], W_TOP, None, ALU.mult))
                nc.vector.tensor_scalar(h_scale[:, :], scale[:, 0:1], H_SCALE, None, ALU.mult)
                nc.vector.tensor_scalar(out_scale[:, :], pow2[:, 0:1], pow2[:, 1:2], None, ALU.mult)
                nc.vector.tensor_scalar(gelu_scale[:, :], pow2[:, 0:1], 1.0 / (W_TOP * LN_SCALE), None, ALU.mult).then_inc(w_scaled, 1)
                dve.wait_ge(w_scaled, 1)
                link(nc.vector.tensor_scalar(out_scale[:, :], out_scale[:, :], 0.5 / (W_TOP * W_TOP * H_SCALE * Y_SCALE), None, ALU.mult))

            softmax_topk(0, weight_scales)
            dve.wait_ge(w_high, 1)
            nc.vector.scalar_tensor_tensor(w1s[:, 1, :, :], w1f[:, :, :], scale[:, 0:1], w1s[:, 0, :, :],
                                           ALU.mult, ALU.subtract).then_inc(w1_split, 1)
            dve.wait_ge(loga_exp, 1)
            nc.vector.memset(decay[:, :], -1.0).then_inc(decay_ready, 1)
            dve.wait_ge(decay_ready, 1)
            link(nc.vector.tensor_scalar(decay[:, :], decay[:, :], exp_a[:, :], None, ALU.mult))
            dve.wait_ge(x_in[1], 16)
            for p in range(NPH):
                build(p, 0)
                build(p, 1)
                with dve.Fori(0, HB // 2 - 1) as i:
                    build(p, 2 * i + 2)
                    low_copy(p, 2 * i, 0)
                    build(p, 2 * i + 3)
                    low_copy(p, 2 * i + 1, 1)
                low_copy(p, HB - 2, 0)
                low_copy(p, HB - 1, 1)

                half, other, nxt = p - 1, (p + 1) % 2, (p + 1) * NCH
                att = half * NCH
                with_att, with_ffn = p in (1, 2), p < NPH - 1
                if with_att:
                    att_stats(half, 0)
                    att_variance()
                    att_norm(att, half, 0)
                h_parts(p, 0, 0)
                h_parts(p, 0, 1)
                if with_att:
                    att_scan(att)
                h_parts(p, 0, 2)
                h_parts(p, 0, 3)
                with chain.loop(0, PAIRS - 1, (4 - len(act_high[p])) + 3 * with_att + 4 * with_ffn) as i:
                    if with_att:
                        att_stats(half, i + 1)
                        att_add(att + i, half, i)
                        att_variance(att + i)
                    if with_ffn:
                        ffn_stats(other, i)
                    h_parts(p, i + 1, 0)
                    if with_ffn:
                        ffn_var()
                    if with_att:
                        att_norm(att + i + 1, half, i + 1)
                    if with_ffn:
                        ffn_norm(nxt + i, other, i)
                    h_parts(p, i + 1, 1)
                    h_parts(p, i + 1, 2)
                    if with_att:
                        att_scan(att + i + 1)
                    y_weigh(p, i, 0)
                    y_weigh(p, i, 1)
                    h_parts(p, i + 1, 3)
                if with_att:
                    att_add(att + NCH - 1, half, NCH - 1)
                    dve.wait_ge(v_added, att + NCH)
                if with_ffn:
                    ffn_stats(other, NCH - 1)
                    ffn_var()
                    ffn_norm(nxt + NCH - 1, other, NCH - 1)
                y_weigh(p, PAIRS - 1, 0)
                y_weigh(p, PAIRS - 1, 1)

                def update(b, p=p):
                    x_update(p, b, b % 2)

                if with_ffn:
                    softmax_topk(p + 1, update)
                else:
                    for b in range(HB):
                        update(b)
                dve.wait_ge(x_updated, CREDIT + (p + 1) * HB)

        @block.tensor
        def _(pe):
            def att_turn(a):
                pe.wait_ge(z_ready, a + 1)
                for t in range(CT):
                    last = nc.tensor.transpose(side[:, t * P:(t + 1) * P], za[:, t, :], ident[:, :])
                last.then_inc(zt_ready, 1)

            def att_in_proj(a):
                pe.wait_ge(zt_copied, a + 1)
                nc.tensor.matmul(side, w_in[:, :], zt[:, :], start=True, stop=True).then_inc(u_ready, 1)

            def att_out_proj(a):
                pe.wait_ge(hseq_ready, a + 1)
                for t in range(CT):
                    last = nc.tensor.matmul(side[:, t * P:(t + 1) * P], hseq[:, t * P:(t + 1) * P], c_mat[:, :],
                                            start=True, stop=True)
                last.then_inc(v_ready, 1)

            def xn_turn(c, i):
                pe.wait_ge(xn_ready, c + 1)
                if not (isinstance(c, int) and c < NCH):
                    pe.wait_ge(y_weighed, 1 + 2 * (c - NCH))
                for t in range(CT):
                    for part in range(2):
                        last = nc.tensor.transpose(xt_bank[:, t, part, :], xn[:, part, i * CT + t, :], ident16[:, :])
                last.then_inc(xt_ready, 1)

            def scores(c, i):
                pe.wait_ge(xt_copied, c + 1)
                for t in range(CT):
                    dst = score[:, t % TH, i * CB + t // TH, :]
                    for k, (a, b) in enumerate(((0, 0), (0, 1), (1, 0))):
                        last = nc.tensor.matmul(dst, xt[:, t, a, :], gws[:, b, :], start=(k == 0), stop=(k == 2))
                last.then_inc(scored, 1)

            def turn_probs(ph):
                pe.wait_ge(probs_ready, ph + 1)
                for h in range(TH):
                    last = nc.tensor.transpose(side[0:RW, h * P:(h + 1) * P],
                                               probs[:, h * HB:(h + 1) * HB, :].rearrange("p b e -> p (b e)"), ident[:, :])
                last.then_inc(pt_turned, 1)

            def turn_topk(ph):
                pe.wait_ge(topk_ready, ph + 1)
                for k, m in enumerate((idx2, top2)):
                    last = nc.tensor.transpose(side[:, k * RW:(k + 1) * RW], m[:, :, :].rearrange("r a s -> r (a s)"),
                                               ident[0:RW, 0:RW])
                last.then_inc(topk_turned, 1)

            def turn_onehot(p, b, k):
                pe.wait_ge(onehot_ready, p * HB + b + 1)
                dst = ps[:, Y_BANK + k, :].bitcast(FP16).rearrange("p (h q s) -> p h q s", h=TH, q=PAIRS)
                for h in range(TH):
                    for q in range(PAIRS):
                        last = nc.tensor.transpose(dst[:, h, q, :], onehot[:, b, q, h * P:(h + 1) * P], ident16[:, :])
                last.then_inc(turned, 1)

            def gather(p, b, k):
                pe.wait_ge(turned_copied, p * HB + b + 1)
                pe.wait_ge(high_copied, p * HB + b + 1)
                pe.wait_ge(low_copied, p * HB + b + 1)
                for part in range(2):
                    for h in range(TH):
                        last = nc.tensor.matmul(ps[:, 2 * k + part, :], xn[:, part, b * TH + h, :], onehot_t[:, k, h, :],
                                                start=(h == 0), stop=(h == TH - 1))
                last.then_inc(gathered, 1)

            def up(p, i, u):
                n = p * UNITS + i * 4 + u
                pe.wait_ge(gelu_done, n + 1)
                e = i * 2 + u // 2
                for j in range(2):
                    cols = slice((2 * (u % 2) + j) * P, (2 * (u % 2) + j + 1) * P)
                    for k, (a, b) in enumerate(((0, 0), (0, 1), (1, 0))):
                        last = nc.tensor.matmul(ps[:, 2 * (u % 2) + j, :], w1s[:, a, e, cols],
                                                xin[:, b, e, :, :].rearrange("p b s -> p (b s)"),
                                                start=(k == 0), stop=(k == 2))
                last.then_inc(up_done, 1)

            def down(p, i, u):
                n = p * UNITS + i * 4 + u
                e = i * 2 + u // 2
                pe.wait_ge(h_low, CREDIT + n + 1)
                if u % 2 == 0:
                    pe.wait_ge(y_copied, p * E + e + 1)
                for j in range(2):
                    for k, (a, b) in enumerate(((0, 0), (1, 0), (0, 1))):
                        last = nc.tensor.matmul(ps[:, Y_BANK, :], w2s[:, a, e, 2 * (u % 2) + j, :],
                                                hs[:, u, b, j * SLOTS:(j + 1) * SLOTS],
                                                start=(u % 2 == 0 and j == 0 and k == 0), stop=(u % 2 == 1 and j == 1 and k == 2))
                if u % 2 == 1:
                    last.then_inc(down_done, 1)

            def turn_y(p, i, g):
                n = (p * PAIRS + i) * 2 + g
                pe.wait_ge(y_copied, 1 + p * E + i * 2 + 2)
                pe.wait_ge(y_weighed, n + 1)
                for b in range(4):
                    last = nc.tensor.transpose(ps[:, TY_BANK, b * P:(b + 1) * P], yt[:, 4 * g + b, :, :].rearrange("p a s -> p (a s)"), ident[:, :])
                last.then_inc(y_turned, 1)

            def scatter(p, b, k):
                pe.wait_ge(x_updated, p * HB + b + 1)
                for h in range(TH):
                    for q in range(PAIRS):
                        for part in range(2):
                            last = nc.tensor.matmul(ps[:, 2 * k, h * C:(h + 1) * C], onehot[:, b, q, h * P:(h + 1) * P],
                                                    ys[:, part, b, q, :], start=(q == 0 and part == 0),
                                                    stop=(q == PAIRS - 1 and part == 1))
                last.then_inc(scattered, 1)

            pe.wait_ge(consts, 3)
            pe.wait_ge(gate_split, 1)
            xn_turn(0, 0)
            for i in range(1, NCH):
                scores(i - 1, i - 1)
                xn_turn(i, i)
            scores(NCH - 1, NCH - 1)
            turn_probs(0)
            turn_topk(0)
            for p in range(NPH):
                turn_onehot(p, 0, 0)
                with pe.Fori(0, HB // 2 - 1) as i:
                    turn_onehot(p, 2 * i + 1, 1)
                    gather(p, 2 * i, 0)
                    turn_onehot(p, 2 * i + 2, 0)
                    gather(p, 2 * i + 1, 1)
                turn_onehot(p, HB - 1, 1)
                gather(p, HB - 2, 0)
                gather(p, HB - 1, 1)

                att, nxt = (p - 1) * NCH, (p + 1) * NCH
                with_att, with_ffn = p in (1, 2), p < NPH - 1
                pe.wait_ge(high_copied, CREDIT + (p + 1) * HB)
                pe.wait_ge(low_copied, CREDIT + (p + 1) * HB)
                pe.wait_ge(w1_split, 1)
                up(p, 0, 0)
                up(p, 0, 1)
                if with_att:
                    pe.wait_ge(att_in, 6 * 16)
                    att_turn(att)
                up(p, 0, 2)
                if with_att:
                    att_in_proj(att)
                up(p, 0, 3)
                pe.wait_ge(w2_split, 1)
                down(p, 0, 0)
                if with_att:
                    att_out_proj(att)
                with pe.Fori(0, PAIRS - 1) as i:
                    up(p, i + 1, 0)
                    down(p, i, 1)
                    up(p, i + 1, 1)
                    down(p, i, 2)
                    up(p, i + 1, 2)
                    if with_att:
                        pe.wait_ge(v_added, att + i + 1)
                        att_turn(att + i + 1)
                    down(p, i, 3)
                    if with_ffn:
                        xn_turn(nxt + i, i)
                    if with_att:
                        att_in_proj(att + i + 1)
                    up(p, i + 1, 3)
                    if with_ffn:
                        pe.wait_ge(xt_copied, nxt + i + 1)
                    turn_y(p, i, 0)
                    if with_ffn:
                        scores(nxt + i, i)
                    down(p, i + 1, 0)
                    if with_att:
                        att_out_proj(att + i + 1)
                    turn_y(p, i, 1)
                for u in range(1, 4):
                    down(p, PAIRS - 1, u)
                if with_ffn:
                    xn_turn(nxt + NCH - 1, NCH - 1)
                    pe.wait_ge(xt_copied, nxt + NCH)
                turn_y(p, PAIRS - 1, 0)
                if with_ffn:
                    scores(nxt + NCH - 1, NCH - 1)
                turn_y(p, PAIRS - 1, 1)

                pe.wait_ge(y_split, CREDIT + (p + 1) * PAIRS * 2)
                with pe.Fori(0, HB // 4) as i:
                    scatter(p, 2 * i, 0)
                    scatter(p, 2 * i + 1, 1)
                if with_ffn:
                    turn_probs(p + 1)
                with pe.Fori(HB // 4, HB // 2) as i:
                    scatter(p, 2 * i, 0)
                    scatter(p, 2 * i + 1, 1)
                if with_ffn:
                    turn_topk(p + 1)


_INS = ['L0_attn_x', 'L0_attn_W_in', 'L0_attn_b_in', 'L0_attn_log_A', 'L0_attn_B_vec', 'L0_attn_C', 'L0_attn_D',
        'L0_ffn_gate_w', 'L0_ffn_w1', 'L0_ffn_w2']


def kernel(**inputs):
    import numpy as _np
    import concourse.bacc as _bacc
    from concourse import mybir as _mybir
    from concourse.bass_utils import run_bass_kernel_spmd as _run

    nc = _bacc.Bacc("TRN2", target_bir_lowering=False, num_devices=1)
    arrays, args = {}, []
    for name in _INS:
        a = _np.ascontiguousarray(inputs[name])
        arrays[f"in_{name}_dram"] = a
        args.append(nc.dram_tensor(f"in_{name}_dram", a.shape, _mybir.dt.from_np(a.dtype), kind="ExternalInput").ap())
    shape = inputs['L0_attn_x'].shape
    out = nc.dram_tensor("out_dram", shape, _mybir.dt.float32, kind="ExternalOutput").ap()
    macaron_kernel(nc, *args, out)
    r = _run(nc, [arrays], core_ids=[0])
    return r.results[0]["out_dram"]
```

```python
import numpy as np
from contextlib import ExitStack, contextmanager

import concourse.bass as bass
from concourse import mybir

FP32 = mybir.dt.float32
FP16 = mybir.dt.float16
INT32 = mybir.dt.int32
UINT32 = mybir.dt.uint32
ALU = mybir.AluOpType
ACT = mybir.ActivationFunctionType
AX = mybir.AxisListType
RED = bass.bass_isa.ReduceOp


class Chain:

    def __init__(self, eng, sem):
        self.eng, self.sem = eng, sem
        self.base, self.local, self.offset = 0, 0, 0

    def counted(self, instruction):
        instruction.then_inc(self.sem, 1)
        self.local += 1

    def hold(self):
        self.eng.wait_ge(self.sem, self.offset + self.base + self.local)

    def link(self, instruction):
        self.counted(instruction)
        self.hold()

    @contextmanager
    def loop(self, start, end, links):
        self.base, self.local = self.base + self.local, 0
        with self.eng.Fori(start, end) as i:
            self.offset = i * links
            self.base -= start * links
            yield i
            assert self.local == links, (self.local, links)
            self.base += start * links
        self.base, self.local, self.offset = self.base + (end - start) * links, 0, 0


def macaron_kernel(nc, x_d, w_in_d, b_in_d, log_a_d, b_vec_d, c_d, d_d, gate_d, w1_d, w2_d, out_d):
    B, T, C = x_d.shape
    E, _, H = w1_d.shape
    P = 128
    TH = T // P
    CAP = 2 * T // E
    HB = B // 2
    NPH = 4
    NCH = 4
    CB = HB // NCH
    CT = CB * TH
    HT = HB * TH
    PAIRS = E // 2
    HC = H // P
    UNITS = 2 * PAIRS * 2
    SLOTS = HB * CAP
    ROUNDS = CAP // 8
    assert C == P and SLOTS == 512 and 2 * CAP == P and HC == 4 and NCH == PAIRS
    EPS = 1e-5
    LN_SCALE = 2.0 ** 10
    GATE_TOP = 2.0 ** 13
    W_TOP = 2.0 ** 15
    H_SCALE = 2.0 ** -4
    Y_SCALE = 2.0 ** -15
    H_CREDIT = 4
    O_CREDIT = 4
    EXP_BITS = 0x7F800000
    act_high = [(0, 2), (0, 1, 2, 3), (0, 1, 2, 3), (0, 1)]
    highs = [0, 8, 24, 40]

    ctx = ExitStack()
    with ctx:
        def sb(name, shape, dt=FP32):
            return ctx.enter_context(nc.sbuf_tensor(name, shape, dt))

        def sem(name):
            return ctx.enter_context(nc.semaphore(name))

        x = sb("x", [P, B * TH, C])
        w1f = sb("w1f", [P, E, H])
        w2f = sb("w2f", [P, E, HC, C])
        hf = w1f[:, :, :].rearrange("p e h -> p (e h)").rearrange("p (u s) -> p u s", u=4)
        w1s = sb("w1s", [P, 2, E, H], FP16)
        w2s = sb("w2s", [P, 2, E, HC, C], FP16)
        gwf = sb("gwf", [P, E])
        gws = sb("gws", [P, 2, E], FP16)
        w_in = sb("w_in", [P, P])
        c_mat = sb("c_mat", [P, P])
        d_row = sb("d_row", [P, C])
        b_in = sb("b_in", [P, 1])
        b_vec = sb("b_vec", [P, 1])
        b_times_b = sb("b_times_b", [P, 1])
        log_a = sb("log_a", [P, 1])
        exp_a = sb("exp_a", [P, 1])
        decay = sb("decay", [P, T])
        ident = sb("ident", [P, P])
        ident16 = sb("ident16", [P, P], FP16)
        iota = sb("iota", [P, T], FP16)
        half_neg = sb("half_neg", [P, HT])
        amax = sb("amax", [P, 4])
        amax_all = sb("amax_all", [P, 4])
        pow2 = sb("pow2", [P, 4])
        scale = sb("scale", [P, 4])
        gelu_scale = sb("gelu_scale", [P, 1])
        h_scale = sb("h_scale", [P, 1])
        exp_scale = sb("exp_scale", [P, 1])
        out_scale = sb("out_scale", [P, 1])

        stats = sb("stats", [P, NCH, CT, 6])
        mv = sb("mv", [P, NCH, CT, 2])
        var_eps = sb("var_eps", [P, NCH, CT])
        rstd = sb("rstd", [P, NCH, CT])
        stats_a = sb("stats_a", [P, HT, 6])
        mv_a = sb("mv_a", [P, HT, 2])
        var_eps_a = sb("var_eps_a", [P, HT])
        rstd_a = sb("rstd_a", [P, HT])
        carrier = sb("carrier", [P, 1])
        act_spare = sb("act_spare", [P, 1])
        zf = sb("zf", [P, CT, C])
        xn = sb("xn", [P, 2, HT, C], FP16)
        xt = sb("xt", [P, 2, CT, 2, P], FP16)
        za = sb("za", [P, CT, C])
        zd = sb("zd", [P, CT, C])
        zt = sb("zt", [P, CT * P])
        bt = sb("bt", [P, CT * P])
        hseq = sb("hseq", [P, CT * P])

        smax = sb("smax", [P, HT])
        sdiff = sb("sdiff", [P, HT, E])
        sexp = sb("sexp", [P, HT, E])
        ssum = sb("ssum", [P, HT])
        srec = sb("srec", [P, HT])
        xo = sb("xo", [P, O_CREDIT, TH, C])
        probs = sb("probs", [P, HT, E])
        RW = HB * E
        ranked = sb("ranked", [RW, T])
        top = sb("top", [RW, CAP])
        idx = sb("idx", [RW, CAP], UINT32)
        top2 = sb("top2", [RW, 2, CAP])
        idx2 = sb("idx2", [RW, 2, CAP])
        idx_s = sb("idx_s", [P, PAIRS, HB])
        top_s = sb("top_s", [P, PAIRS, HB])

        onehot = sb("onehot", [P, HB, PAIRS, T], FP16)
        onehot_t = sb("onehot_t", [P, 2, TH, PAIRS * P], FP16)
        xin = sb("xin", [P, 2, E, HB, CAP], FP16)
        hs = sb("hs", [P, 4, 2, 2 * SLOTS], FP16)
        yt = sb("yt", [P, HB, 2, CAP])
        yf = sb("yf", [P, 2, 4, C])
        ys = sb("ys", [P, 2, HB, PAIRS, C], FP16)

        ps = ctx.enter_context(nc.psum_tensor("ps", [P, 8, 512], FP32))
        Y_BANK, TY_BANK, SIDE_BANK, SCORE_BANK = 4, 5, 6, 7
        FINAL_BANKS = [0, 1, 2, 3, SIDE_BANK, SCORE_BANK, 0, 1]
        side = ps[:, SIDE_BANK, :]
        xt_banks = [ps[:, bank, :].bitcast(FP16).rearrange("p (t s c) -> p t s c", t=CT, s=2) for bank in (TY_BANK, Y_BANK)]
        gram = ps[:, 0, 0:C]
        score = ps[:, SCORE_BANK, 0:HT * E].rearrange("p (h b e) -> p h b e", h=TH, e=E)

        x_in = [sem(f"x_in{k}") for k in range(NCH + 1)]
        gate_in, w1_in, w2_in, att_in = sem("gate_in"), sem("w1_in"), sem("w2_in"), sem("att_in")
        consts = sem("consts")
        gate_max, gate_shared, gate_scaled = sem("gate_max"), sem("gate_shared"), sem("gate_scaled")
        w1_squares, w2_gram, w2_squares = sem("w1_squares"), sem("w2_gram"), sem("w2_squares")
        w_shared, w_scaled = sem("w_shared"), sem("w_scaled")
        w_high, w1_split, w2_split = sem("w_high"), sem("w1_split"), sem("w2_split")
        gate_high, gate_split = sem("gate_high"), sem("gate_split")
        loga_exp = sem("loga_exp")
        dve_chain, act_chain, pool_chain = sem("dve_chain"), sem("act_chain"), sem("pool_chain")
        ln_var, ln_rstd, xn_high = sem("ln_var"), sem("ln_rstd"), sem("xn_high")
        xn_ready, xn_last = sem("xn_ready"), sem("xn_last")
        xt_ready, xt_copied, scored = sem("xt_ready"), sem("xt_copied"), sem("scored")
        sdiff_ready, sexp_ready, probs_ready = sem("sdiff_ready"), sem("sexp_ready"), sem("probs_ready")
        pt_turned, topk_ready, topk_turned = sem("pt_turned"), sem("topk_ready"), sem("topk_turned")
        onehot_ready, turned, turned_copied = sem("onehot_ready"), sem("turned"), sem("turned_copied")
        gathered, high_copied, low_copied = sem("gathered"), sem("high_copied"), sem("low_copied")
        up_done, gelu_done, h_high, h_low = sem("up_done"), sem("gelu_done"), sem("h_high"), sem("h_low")
        down_done, y_copied = sem("down_done"), sem("y_copied")
        y_turned, y_weighed, y_high, y_split = sem("y_turned"), sem("y_weighed"), sem("y_high"), sem("y_split")
        y_final, x_final = sem("y_final"), sem("x_final")
        scattered, o_copied, x_updated = sem("scattered"), sem("o_copied"), sem("x_updated")
        att_var, att_rstd, z_ready, xd_added = sem("att_var"), sem("att_rstd"), sem("z_ready"), sem("xd_added")
        zt_ready, zt_copied, u_ready, bt_ready = sem("zt_ready"), sem("zt_copied"), sem("u_ready"), sem("bt_ready")
        hseq_ready, v_ready, v_added = sem("hseq_ready"), sem("v_ready"), sem("v_added")
        out_sent = sem("out_sent")

        CREDIT = 2

        def tiles_of(half, i):
            return bass.ds(half * HT + i * CT, CT) if not isinstance(i, int) else slice(half * HT + i * CT, half * HT + (i + 1) * CT)

        def at(i, n):
            return bass.ds(i, n) if not isinstance(i, int) else slice(i, i + n)

        def att_part(part):
            return slice(0, CT) if part == 0 else slice(CT, HT)

        block = ctx.enter_context(nc.Block())

        @block.sync
        def _(sp):
            xv = x_d.rearrange("b (h p) c -> p (b h) c", p=P)
            ov = out_d.rearrange("b (h p) c -> p (b h) c", p=P)
            q = HT // 2
            sp.dma_start(gwf[:, :], gate_d).then_inc(gate_in, 16)
            for k in range(NCH):
                sp.dma_start(x[:, k * CT:(k + 1) * CT, :], xv[:, k * CT:(k + 1) * CT, :]).then_inc(x_in[k], 16)
            sp.dma_start(w1f[:, :, :], w1_d.rearrange("e c h -> c e h")).then_inc(w1_in, 16)
            sp.dma_start(w2f[:, :, :, :], w2_d.rearrange("e (k p) c -> p e k c", p=P)).then_inc(w2_in, 16)
            sp.dma_start(x[:, HT:2 * HT, :], xv[:, HT:2 * HT, :]).then_inc(x_in[NCH], 16)
            sp.dma_start(w_in[:, :], w_in_d).then_inc(att_in, 16)
            sp.dma_start(c_mat[:, :], c_d).then_inc(att_in, 16)
            sp.dma_start(d_row[:, :], d_d.rearrange("(a c) -> a c", a=1).broadcast_to([P, C])).then_inc(att_in, 16)
            for dst, src in ((b_in, b_in_d), (b_vec, b_vec_d), (log_a, log_a_d)):
                sp.dma_start(dst[:, :], src.rearrange("(c a) -> c a", a=1)).then_inc(att_in, 16)
            for k in range(2):
                sp.wait_ge(x_updated, O_CREDIT + 2 * HB + (k + 1) * HB // 2)
                sp.dma_start(ov[:, k * q:(k + 1) * q, :], x[:, k * q:(k + 1) * q, :]).then_inc(out_sent, 16)
            for i in range(NCH):
                sp.wait_ge(x_final, (i + 1) * CB)
                lo = HT + i * CT
                sp.dma_start(ov[:, lo:lo + CT, :], x[:, lo:lo + CT, :]).then_inc(out_sent, 16)
            sp.wait_ge(out_sent, (2 + NCH) * 16)

        @block.gpsimd
        def _(pool):
            chain = Chain(pool, pool_chain)
            chain.link(nc.gpsimd.memset(ident[:, :], 0.0))
            chain.link(nc.gpsimd.affine_select(out=ident[:, :], in_=ident[:, :], compare_op=ALU.not_equal,
                                               fill=1.0, base=0, pattern=[[-1, P]], channel_multiplier=1))
            nc.gpsimd.tensor_copy(ident16[:, :], ident[:, :]).then_inc(consts, 1)
            nc.gpsimd.memset(half_neg[:, :], -0.5).then_inc(consts, 1)
            nc.gpsimd.iota(iota[:, :], pattern=[[1, T]], base=0, channel_multiplier=0,
                           allow_small_or_imprecise_dtypes=True).then_inc(consts, 1)
            pool.wait_ge(consts, 3)

            def ffn_rstd(c, k=0):
                pool.wait_ge(ln_var, c + 1)
                nc.gpsimd.tensor_tensor(rstd[:, k, :], var_eps[:, k, :], half_neg[:, 0:CT], ALU.pow).then_inc(ln_rstd, 1)

            def att_rstd_pool(p, part):
                pool.wait_ge(att_var, (p - 1) * 2 + part + 1)
                t = att_part(part)
                nc.gpsimd.tensor_tensor(rstd_a[:, t], var_eps_a[:, t], half_neg[:, t], ALU.pow).then_inc(att_rstd, 1)

            def att_skip(a, half, i):
                pool.wait_ge(z_ready, a + 1)
                if not (isinstance(a, int) and a == 0):
                    pool.wait_ge(xd_added, a)
                tiles = tiles_of(half, i)
                chain.link(nc.gpsimd.tensor_tensor(zd[:, :, :], za[:, :, :],
                                                   d_row[:, :].unsqueeze(1).broadcast_to([P, CT, C]), ALU.mult))
                nc.gpsimd.tensor_tensor(x[:, tiles, :], x[:, tiles, :], zd[:, :, :], ALU.add).then_inc(xd_added, 1)

            def xn_part(c, i, z=zf):
                pool.wait_ge(xn_high, c + 1)
                hi, lo = (xn[:, part, at(i * CT, CT), :] for part in range(2))
                nc.gpsimd.tensor_tensor(lo, z[:, :, :], hi, ALU.subtract).then_inc(xn_ready, 1)

            def y_low(p, i):
                for g in range(2):
                    pool.wait_ge(y_high, (p * PAIRS + i) * 2 + g + 1)
                    hi, lo = (ys[:, part, 4 * g:4 * g + 4, at(i, 1), :] for part in range(2))
                    nc.gpsimd.tensor_tensor(lo, yf[:, g, :, :].unsqueeze(2), hi, ALU.subtract).then_inc(y_split, 1)

            def x_update(p, b, k):
                pool.wait_ge(o_copied, O_CREDIT + p * HB + b + 1)
                xs = x[:, at((p % 2) * HT + b * TH, TH), :]
                nc.gpsimd.tensor_tensor(xs, xs, xo[:, k, :, :], ALU.add).then_inc(x_updated, 1)

            pool.nop().then_inc(y_split, CREDIT)
            pool.nop().then_inc(x_updated, O_CREDIT)
            pool.wait_ge(gate_max, 1)
            nc.gpsimd.partition_all_reduce(amax_all[:, 2:3], amax[:, 2:3], P, RED.max).then_inc(gate_shared, 1)
            for i in range(NCH):
                ffn_rstd(i, i)
                if i >= 1:
                    xn_part(i - 1, i - 1, za if i % 2 == 0 else zf)
            xn_part(NCH - 1, NCH - 1, za)
            for k, squares in enumerate((w1_squares, w2_squares)):
                pool.wait_ge(squares, 1)
                nc.gpsimd.partition_all_reduce(amax_all[:, k:k + 1], amax[:, k:k + 1], P, RED.add).then_inc(w_shared, 1)
            pool.wait_ge(w_high, 1)
            nc.gpsimd.tensor_tensor(w1s[:, 1, :, :], w1f[:, :, :], w1s[:, 0, :, :], ALU.subtract).then_inc(w1_split, 1)
            pool.wait_ge(w_high, 2)
            nc.gpsimd.tensor_tensor(w2s[:, 1, :, :, :], w2f[:, :, :, :], w2s[:, 0, :, :, :], ALU.subtract).then_inc(w2_split, 1)
            for p in range(NPH):
                half, nxt = p - 1, (p + 1) * NCH
                with_att, with_ffn = p in (1, 2), p < NPH - 1
                if with_att:
                    att_rstd_pool(p, 0)
                    att_skip(half * NCH, half, 0)
                    att_rstd_pool(p, 1)
                if with_ffn:
                    ffn_rstd(nxt)
                with pool.Fori(0, PAIRS - 1) if not with_att else chain.loop(0, PAIRS - 1, 1) as i:
                    if with_ffn:
                        xn_part(nxt + i, i)
                    if with_att:
                        att_skip(half * NCH + i + 1, half, i + 1)
                    if with_ffn:
                        ffn_rstd(nxt + i + 1)
                    y_low(p, i)
                if with_ffn:
                    y_low(p, PAIRS - 1)
                    for b in range(HB):
                        x_update(p, b, b % O_CREDIT)

        @block.scalar
        def _(act):
            chain = Chain(act, act_chain)

            def tables(function):
                nc.scalar.activation(act_spare[:, :], half_neg[:, 0:1], function)

            def xt_copy(c, k=0):
                act.wait_ge(xt_ready, c + 1)
                nc.scalar.copy(xt[:, k, :, :, :], xt_banks[k]).then_inc(xt_copied, 1)

            def zt_copy(a):
                act.wait_ge(zt_ready, a + 1)
                nc.scalar.copy(zt[:, :], side).then_inc(zt_copied, 1)

            def bt_make(a):
                act.wait_ge(u_ready, a + 1)
                if not (isinstance(a, int) and a == 0):
                    act.wait_ge(hseq_ready, a)
                nc.scalar.activation(bt[:, :], side, ACT.Identity, bias=b_times_b[:, :],
                                     scale=b_vec[:, :]).then_inc(bt_ready, 1)

            def softmax_exp(ph):
                act.wait_ge(sdiff_ready, ph + 1)
                nc.scalar.activation(sexp[:, :, :], sdiff[:, :, :], ACT.Exp, scale=exp_scale[:, :]).then_inc(sexp_ready, 1)

            def turned_copy(p, b, k):
                act.wait_ge(turned, p * HB + b + 1)
                if not (p == 0 and isinstance(b, int) and b < 2):
                    act.wait_ge(gathered, p * HB + b - 1)
                nc.scalar.copy(onehot_t[:, k, :, :].rearrange("p h s -> p (h s)"),
                               ps[:, Y_BANK + k, :].bitcast(FP16)).then_inc(turned_copied, 1)

            def high_copy(p, b, k):
                act.wait_ge(gathered, p * HB + b + 1)
                nc.scalar.copy(xin[:, 0, :, at(b, 1), :],
                               ps[:, 2 * k, :].rearrange("p (e o s) -> p e o s", e=E, o=1)).then_inc(high_copied, 1)

            def gelu(p, i, u):
                n = p * UNITS + i * 4 + u
                act.wait_ge(up_done, n + 1)
                act.wait_ge(h_low, n + 1)
                nc.scalar.activation(hf[:, u, :], ps[:, 2 * (u % 2):2 * (u % 2) + 2, :].rearrange("p a b -> p (a b)"),
                                     ACT.Gelu, scale=gelu_scale[:, :]).then_inc(gelu_done, 1)

            def high(p, i, u):
                n = p * UNITS + i * 4 + u
                if u in act_high[p]:
                    act.wait_ge(gelu_done, CREDIT + n + 1)
                    nc.scalar.activation(hs[:, u, 0, :], hf[:, u, :], ACT.Copy, scale=h_scale[:, :]).then_inc(h_high, 1)

            def y_high_copy(p, i):
                for g in range(2):
                    act.wait_ge(y_weighed, CREDIT + (p * PAIRS + i) * 2 + g + 1)
                    nc.scalar.copy(ys[:, 0, 4 * g:4 * g + 4, at(i, 1), :], yf[:, g, :, :].unsqueeze(2)).then_inc(y_high, 1)

            def y_copy(p, i, k):
                act.wait_ge(down_done, p * E + i * 2 + k + 1)
                nc.scalar.copy(yt[:, :, k, :], ps[:, Y_BANK, :].rearrange("p (b s) -> p b s", b=HB)).then_inc(y_copied, 1)

            def o_copy(p, b, k):
                act.wait_ge(scattered, p * HB + b + 1)
                act.wait_ge(x_updated, p * HB + b + 1)
                nc.scalar.activation(xo[:, k, :, :], ps[:, k, 0:TH * C].rearrange("p (h c) -> p h c", h=TH), ACT.Copy,
                                     scale=out_scale[:, :]).then_inc(o_copied, 1)

            act.nop().then_inc(o_copied, O_CREDIT)
            act.nop().then_inc(high_copied, CREDIT)
            act.nop().then_inc(gelu_done, CREDIT)
            act.nop().then_inc(y_copied, 1)
            act.wait_ge(gate_scaled, 1)
            nc.scalar.activation(gws[:, 0, :], gwf[:, :], ACT.Copy, scale=scale[:, 2:3]).then_inc(gate_high, 1)
            junk = hs[:, :, :, :].rearrange("p u a s -> p (u a s)")[:, 0:E * H]
            xt_copy(0)
            act.wait_ge(w1_in, 16)
            nc.scalar.activation(junk, w1f[:, :, :].rearrange("p e h -> p (e h)"), ACT.Square,
                                 accum_out=amax[:, 0:1]).then_inc(w1_squares, 1)
            for i in range(1, NCH):
                if i >= 2:
                    act.wait_ge(scored, i - 1)
                xt_copy(i, i % 2)
            softmax_exp(0)
            act.wait_ge(att_in, 6 * 16)
            nc.scalar.activation(exp_a[:, :], log_a[:, :], ACT.Exp).then_inc(loga_exp, 1)
            for k, (wf, ws) in enumerate(((w1f[:, :, :], w1s[:, 0, :, :]), (w2f[:, :, :, :], w2s[:, 0, :, :, :]))):
                act.wait_ge(w_scaled, k + 1)
                chain.link(nc.scalar.activation(wf, wf, ACT.Copy, scale=scale[:, k:k + 1]))
                nc.scalar.copy(ws, wf).then_inc(w_high, 1)
            for p in range(NPH):
                turned_copy(p, 0, 0)
                turned_copy(p, 1, 1)
                with act.Fori(0, HB // 2 - 1) as i:
                    high_copy(p, 2 * i, 0)
                    turned_copy(p, 2 * i + 2, 0)
                    high_copy(p, 2 * i + 1, 1)
                    turned_copy(p, 2 * i + 3, 1)
                high_copy(p, HB - 2, 0)
                high_copy(p, HB - 1, 1)

                att, nxt = (p - 1) * NCH, (p + 1) * NCH
                with_att, with_ffn = p in (1, 2), p < NPH - 1
                gelu(p, 0, 0)
                if with_att:
                    zt_copy(att)
                high(p, 0, 0)
                gelu(p, 0, 1)
                if with_att:
                    bt_make(att)
                high(p, 0, 1)
                for u in range(2, 4):
                    gelu(p, 0, u)
                    high(p, 0, u)
                with act.Fori(0, PAIRS - 1) as i:
                    gelu(p, i + 1, 0)
                    y_copy(p, i, 0)
                    if with_att:
                        zt_copy(att + i + 1)
                    high(p, i + 1, 0)
                    gelu(p, i + 1, 1)
                    if with_att:
                        bt_make(att + i + 1)
                    high(p, i + 1, 1)
                    gelu(p, i + 1, 2)
                    if with_ffn:
                        xt_copy(nxt + i)
                    high(p, i + 1, 2)
                    y_copy(p, i, 1)
                    gelu(p, i + 1, 3)
                    high(p, i + 1, 3)
                    y_high_copy(p, i)
                y_copy(p, PAIRS - 1, 0)
                if with_ffn:
                    tables(ACT.Exp)
                    xt_copy(nxt + NCH - 1)
                    softmax_exp(p + 1)
                y_copy(p, PAIRS - 1, 1)
                y_high_copy(p, PAIRS - 1)
                if with_ffn:
                    for b in range(HB):
                        o_copy(p, b, b % O_CREDIT)
                    tables(ACT.Gelu)

        @block.vector
        def _(dve):
            chain = Chain(dve, dve_chain)
            link = chain.link

            def carry():
                nc.vector.tensor_scalar(carrier[:, :], half_neg[:, 0:1], 1.0, None, ALU.mult)

            def statistics(tile, st):
                for t in range(st.shape[1]):
                    last = nc.vector.bn_stats(st[:, t, :], x[:, tile + t, :])
                link(last)

            def variance(st, m, ve, ready, scale=1.0):
                for t in range(st.shape[1]):
                    last = nc.vector.bn_aggr(m[:, t, :], st[:, t, :])
                link(last)
                nc.vector.tensor_scalar(ve, m[:, :, 1], EPS, scale, ALU.add, ALU.mult).then_inc(ready, 1)

            def normalise(half, i, m, r, z, first=0):
                for t in range(CT):
                    last = nc.vector.tensor_scalar(z[:, t, :], x[:, half * HT + i * CT + t, :], m[:, at(first + t, 1), 0],
                                                   r[:, at(first + t, 1)], ALU.subtract, ALU.mult)
                return last

            def ffn_stats(half, i, k=0):
                statistics(half * HT + i * CT, stats[:, k])

            def ffn_var(k=0):
                variance(stats[:, k], mv[:, k], var_eps[:, k, :], ln_var, LN_SCALE ** -2)

            def ffn_norm(c, half, i, k=0, z=zf, p=0):
                dve.wait_ge(ln_rstd, c + 1)
                if not isinstance(c, int):
                    dve.wait_ge(xn_ready, NCH + p * (NCH - 1) + i)
                elif c >= NCH:
                    dve.wait_ge(xn_ready, NCH + (p + 1) * (NCH - 1))
                elif c >= 2:
                    dve.wait_ge(xn_ready, c - 1)
                link(normalise(half, i, mv[:, k], rstd[:, k, :], z))
                nc.vector.tensor_copy(xn[:, 0, at(i * CT, CT), :], z[:, :, :]).then_inc(xn_high, 1)

            def xn_low(p, i):
                dve.wait_ge(xn_high, (p + 2) * NCH)
                hi, lo = (xn[:, part, i * CT:(i + 1) * CT, :] for part in range(2))
                nc.vector.tensor_tensor(lo, zf[:, :, :], hi, ALU.subtract).then_inc(xn_last, 1)
                dve.wait_ge(xn_last, p + 1)

            def att_stats(half, part):
                t = att_part(part)
                statistics(half * HT + t.start, stats_a[:, t])
                variance(stats_a[:, t], mv_a[:, t], var_eps_a[:, t], att_var)

            def att_norm(a, half, i):
                if isinstance(i, int):
                    dve.wait_ge(att_rstd, half * 2 + 1)
                else:
                    dve.wait_ge(att_rstd, half * 2 + 2)
                if not (isinstance(a, int) and a == 0):
                    dve.wait_ge(xd_added, a)
                    dve.wait_ge(zt_ready, a)
                normalise(half, i, mv_a, rstd_a, za, i * CT).then_inc(z_ready, 1)

            def scan_constants():
                dve.wait_ge(loga_exp, 1)
                link(nc.vector.memset(decay[:, :], -1.0))
                nc.vector.tensor_scalar(b_times_b[:, :], b_in[:, :], b_vec[:, :], None, ALU.mult)
                link(nc.vector.tensor_scalar(decay[:, :], decay[:, :], exp_a[:, :], None, ALU.mult))

            def att_scan(a):
                dve.wait_ge(bt_ready, a + 1)
                for b in range(CB):
                    rows = slice(b * T, (b + 1) * T)
                    last = nc.vector.tensor_tensor_scan(hseq[:, rows], decay[:, :], bt[:, rows], 0.0, ALU.mult, ALU.add)
                last.then_inc(hseq_ready, 1)

            def att_add(a, half, i):
                dve.wait_ge(v_ready, a + 1)
                dve.wait_ge(xd_added, a + 1)
                xs = x[:, tiles_of(half, i), :]
                nc.vector.tensor_tensor(xs, side.rearrange("p (t c) -> p t c", t=CT), xs, ALU.add).then_inc(v_added, 1)

            def softmax_diff(ph):
                dve.wait_ge(scored, (ph + 1) * NCH)
                sc = score.rearrange("p h b e -> p (h b) e")
                link(nc.vector.tensor_reduce(smax[:, :], sc, AX.X, ALU.max))
                nc.vector.tensor_tensor(sdiff[:, :, :], sc, smax[:, :].unsqueeze(2).broadcast_to([P, HT, E]),
                                        ALU.subtract).then_inc(sdiff_ready, 1)

            def softmax_probs(ph):
                dve.wait_ge(sexp_ready, ph + 1)
                link(nc.vector.tensor_reduce(ssum[:, :], sexp[:, :, :], AX.X, ALU.add))
                link(nc.vector.reciprocal(srec[:, :], ssum[:, :]))
                nc.vector.tensor_tensor(probs[:, :, :], sexp[:, :, :], srec[:, :].unsqueeze(2).broadcast_to([P, HT, E]),
                                        ALU.mult).then_inc(probs_ready, 1)

            def topk(ph, meanwhile={}):
                dve.wait_ge(pt_turned, ph + 1)
                link(nc.vector.tensor_copy(ranked[:, :], side[0:RW, 0:T]))
                def keep(r):
                    cols = slice(8 * r, 8 * r + 8)
                    nc.vector.tensor_copy(idx2[:, :, cols], idx[:, cols].unsqueeze(1).broadcast_to([RW, 2, 8]))
                    return nc.vector.tensor_scalar(top2[:, :, cols], top[:, cols].unsqueeze(1).broadcast_to([RW, 2, 8]),
                                                   Y_SCALE, None, ALU.mult)

                for r in range(ROUNDS):
                    best = top[:, 8 * r:8 * r + 8]
                    chain.counted(nc.vector.max(best, ranked[:, :]))
                    if r > 0:
                        keep(r - 1)
                    chain.hold()
                    found = nc.vector.max_index(idx[:, 8 * r:8 * r + 8], best, ranked[:, :])
                    if r in meanwhile:
                        meanwhile[r]()
                    if r < ROUNDS - 1:
                        found = nc.vector.match_replace(ranked[:, :], best, ranked[:, :], -1.0)
                    link(found)
                keep(ROUNDS - 1).then_inc(topk_ready, 1)
                dve.wait_ge(topk_turned, ph + 1)
                for dst, at0 in ((idx_s, 0), (top_s, RW)):
                    src = side[:, at0:at0 + RW].rearrange("p (b q o) -> p o q b", q=PAIRS, o=2)
                    for par in range(2):
                        rows = slice(par * CAP, (par + 1) * CAP)
                        last = nc.vector.tensor_copy(dst[rows, :, :], src[rows, par, :, :])
                link(last)

            def build(p, b):
                for q in range(PAIRS):
                    last = nc.vector.tensor_scalar(onehot[:, at(b, 1), q, :], iota[:, :].unsqueeze(1),
                                                   idx_s[:, q, at(b, 1)], None, ALU.is_equal)
                last.then_inc(onehot_ready, 1)

            def low_copy(p, b, k):
                dve.wait_ge(gathered, p * HB + b + 1)
                nc.vector.tensor_scalar(xin[:, 1, :, at(b, 1), :],
                                        ps[:, 2 * k + 1, :].rearrange("p (e o s) -> p e o s", e=E, o=1),
                                        1.0, None, ALU.mult).then_inc(low_copied, 1)

            def h_parts(p, i, u):
                n = p * UNITS + i * 4 + u
                if u not in act_high[p]:
                    dve.wait_ge(gelu_done, CREDIT + n + 1)
                    link(nc.vector.tensor_scalar(hs[:, u, 0, :], hf[:, u, :], h_scale[:, :], None, ALU.mult))
                else:
                    dve.wait_ge(h_high, highs[p] + i * len(act_high[p]) + act_high[p].index(u) + 1)
                nc.vector.scalar_tensor_tensor(hs[:, u, 1, :], hf[:, u, :], h_scale[:, :], hs[:, u, 0, :],
                                               ALU.mult, ALU.subtract).then_inc(h_low, 1)

            def y_weigh(p, i, g, bank=TY_BANK):
                n = (p * PAIRS + i) * 2 + g
                dve.wait_ge(y_turned, n + 1)
                dve.wait_ge(y_split, n + 1)
                nc.vector.tensor_tensor(yf[:, g, :, :], ps[:, bank, :].rearrange("p (b c) -> p b c", b=4),
                                        top_s[:, at(i, 1), 4 * g:4 * g + 4].rearrange("p o b -> p (o b)").unsqueeze(2).broadcast_to([P, 4, C]),
                                        ALU.mult).then_inc(y_weighed, 1)

            def y_low_final(p, g):
                dve.wait_ge(y_high, (p * PAIRS + PAIRS - 1) * 2 + g + 1)
                hi, lo = (ys[:, part, 4 * g:4 * g + 4, PAIRS - 1, :] for part in range(2))
                nc.vector.tensor_tensor(lo, yf[:, g, :, :], hi, ALU.subtract).then_inc(y_final, 1)

            def x_update_final(p, b):
                dve.wait_ge(scattered, p * HB + b + 1)
                xs = x[:, (p % 2) * HT + b * TH:(p % 2) * HT + (b + 1) * TH, :]
                nc.vector.scalar_tensor_tensor(xs, ps[:, FINAL_BANKS[b], 0:TH * C].rearrange("p (h c) -> p h c", h=TH),
                                               out_scale[:, :], xs, ALU.mult, ALU.add).then_inc(x_final, 1)

            dve.nop().then_inc(low_copied, CREDIT)
            dve.nop().then_inc(h_low, H_CREDIT)
            dve.nop().then_inc(y_weighed, CREDIT)

            def pow2_scale(cols):
                link(nc.vector.tensor_scalar(pow2[:, cols].bitcast(INT32), amax_all[:, cols].bitcast(INT32),
                                             EXP_BITS, None, ALU.bitwise_and))
                link(nc.vector.tensor_scalar(pow2[:, cols], pow2[:, cols], 2.0 ** -60, None, ALU.max))
                link(nc.vector.reciprocal(scale[:, cols], pow2[:, cols]))
                link(nc.vector.tensor_scalar(scale[:, cols], scale[:, cols], GATE_TOP, None, ALU.mult))

            dve.wait_ge(gate_in, 16)
            nc.vector.tensor_reduce(amax[:, 2:3], gwf[:, :], AX.X, ALU.max, apply_absolute_value=True).then_inc(gate_max, 1)
            dve.wait_ge(gate_shared, 1)
            pow2_scale(slice(2, 3))
            nc.vector.tensor_scalar(exp_scale[:, :], pow2[:, 2:3], 1.0 / (GATE_TOP * LN_SCALE), None, ALU.mult).then_inc(gate_scaled, 1)
            def weight_scale(k):
                dve.wait_ge(w_shared, k + 1)
                w, pw, sc = amax_all[:, k:k + 1], pow2[:, k:k + 1], scale[:, k:k + 1]
                link(nc.vector.tensor_scalar(w, w, 2.0 ** -100, 2.0 ** 100, ALU.max, ALU.min))
                link(nc.vector.tensor_scalar(pw.bitcast(INT32), w.bitcast(INT32), 1, EXP_BITS,
                                             ALU.logical_shift_right, ALU.bitwise_and))
                link(nc.vector.tensor_scalar(pw, pw, 2.0 ** 64, None, ALU.mult))
                link(nc.vector.reciprocal(sc, pw))
                link(nc.vector.tensor_scalar(sc, sc, W_TOP, None, ALU.mult))
                if k == 0:
                    nc.vector.tensor_scalar(h_scale[:, :], sc, H_SCALE, None, ALU.mult)
                    nc.vector.tensor_scalar(gelu_scale[:, :], pw, 1.0 / (W_TOP * LN_SCALE), None, ALU.mult).then_inc(w_scaled, 1)
                else:
                    link(nc.vector.tensor_scalar(out_scale[:, :], pow2[:, 0:1], pw, None, ALU.mult))
                    nc.vector.tensor_scalar(out_scale[:, :], out_scale[:, :], 0.5 / (W_TOP * W_TOP * H_SCALE * Y_SCALE),
                                            None, ALU.mult).then_inc(w_scaled, 1)

            def w2_square_sum():
                dve.wait_ge(w2_gram, 1)
                link(nc.vector.tensor_tensor(hseq[:, 0:C], gram, ident[:, :], ALU.mult))
                nc.vector.tensor_reduce(amax[:, 1:2], hseq[:, 0:C], AX.X, ALU.add).then_inc(w2_squares, 1)

            def first_norm(i):
                ffn_norm(i, 0, i, i, za if i % 2 else zf)

            for i in range(NCH):
                dve.wait_ge(x_in[i], 16)
                ffn_stats(0, i, i)
                ffn_var(i)
                if i == 1:
                    dve.wait_ge(gate_high, 1)
                    nc.vector.scalar_tensor_tensor(gws[:, 1, :], gwf[:, :], scale[:, 2:3], gws[:, 0, :],
                                                   ALU.mult, ALU.subtract).then_inc(gate_split, 1)
                if i >= 1:
                    first_norm(i - 1)
            first_norm(NCH - 1)
            weight_scale(0)
            softmax_diff(0)
            softmax_probs(0)
            topk(0, {3: w2_square_sum, 4: lambda: weight_scale(1)})
            dve.wait_ge(x_in[NCH], 16)
            for p in range(NPH):
                for b in range(HB // 2):
                    build(p, b)
                with dve.Fori(0, HB // 4) as i:
                    low_copy(p, 2 * i, 0)
                    build(p, 2 * i + HB // 2)
                    low_copy(p, 2 * i + 1, 1)
                    build(p, 2 * i + 1 + HB // 2)
                low_copy(p, HB // 2, 0)
                low_copy(p, HB // 2 + 1, 1)
                half, other, nxt = p - 1, (p + 1) % 2, (p + 1) * NCH
                att = half * NCH
                with_att, with_ffn = p in (1, 2), p < NPH - 1
                if p == 0:
                    scan_constants()
                if with_att:
                    att_stats(half, 0)
                low_copy(p, HB - 2, 0)
                if with_att:
                    low_copy(p, HB - 1, 1)
                    att_norm(att, half, 0)
                else:
                    low_copy(p, HB - 1, 1)
                if with_att:
                    att_stats(half, 1)
                h_parts(p, 0, 0)
                if with_att:
                    att_scan(att)
                h_parts(p, 0, 1)
                if with_att:
                    att_add(att, half, 0)
                    dve.wait_ge(v_added, att + 1)
                if with_ffn:
                    ffn_stats(other, 0)
                    ffn_var()
                h_parts(p, 0, 2)
                with chain.loop(0, PAIRS - 1, (4 - len(act_high[p])) + 3 * with_ffn) as i:
                    if with_att:
                        att_norm(att + i + 1, half, i + 1)
                    h_parts(p, i, 3)
                    if with_ffn:
                        ffn_norm(nxt + i, other, i, p=p)
                    h_parts(p, i + 1, 0)
                    if with_att:
                        att_scan(att + i + 1)
                    h_parts(p, i + 1, 1)
                    if with_att:
                        att_add(att + i + 1, half, i + 1)
                        dve.wait_ge(v_added, att + i + 2)
                        carry()
                    if with_ffn:
                        ffn_stats(other, i + 1)
                        carry()
                        ffn_var()
                    h_parts(p, i + 1, 2)
                    y_weigh(p, i, 0)
                    y_weigh(p, i, 1, SIDE_BANK)
                if with_ffn:
                    ffn_norm(nxt + NCH - 1, other, NCH - 1, p=p)
                    xn_low(p, NCH - 1)
                h_parts(p, PAIRS - 1, 3)
                if with_ffn:
                    softmax_diff(p + 1)
                if with_ffn:
                    softmax_probs(p + 1)
                    topk(p + 1, {0: lambda: y_weigh(p, PAIRS - 1, 0), 1: lambda: y_weigh(p, PAIRS - 1, 1, Y_BANK)})
                else:
                    y_weigh(p, PAIRS - 1, 0)
                    y_weigh(p, PAIRS - 1, 1, Y_BANK)
                    for g in range(2):
                        y_low_final(p, g)
                    for b in range(HB):
                        x_update_final(p, b)
                if with_ffn:
                    dve.wait_ge(x_updated, O_CREDIT + (p + 1) * HB)

        @block.tensor
        def _(pe):
            def att_turn(a):
                pe.wait_ge(z_ready, a + 1)
                for t in range(CT):
                    last = nc.tensor.transpose(side[:, t * P:(t + 1) * P], za[:, t, :], ident[:, :])
                last.then_inc(zt_ready, 1)

            def att_in_proj(a):
                pe.wait_ge(zt_copied, a + 1)
                nc.tensor.matmul(side, w_in[:, :], zt[:, :], start=True, stop=True).then_inc(u_ready, 1)

            def att_out_proj(a):
                pe.wait_ge(hseq_ready, a + 1)
                for t in range(CT):
                    last = nc.tensor.matmul(side[:, t * P:(t + 1) * P], hseq[:, t * P:(t + 1) * P], c_mat[:, :],
                                            start=True, stop=True)
                last.then_inc(v_ready, 1)

            def xn_turn(c, i, k=0, p=0):
                if isinstance(i, int) and c >= NCH:
                    pe.wait_ge(xn_last, c // NCH)
                elif isinstance(i, int):
                    pe.wait_ge(xn_ready, c + 1)
                else:
                    pe.wait_ge(xn_ready, NCH + p * (NCH - 1) + i + 1)
                if not (isinstance(c, int) and c < NCH):
                    pe.wait_ge(y_weighed, CREDIT + 2 * (c - NCH))
                for t in range(CT):
                    for part in range(2):
                        last = nc.tensor.transpose(xt_banks[k][:, t, part, :], xn[:, part, i * CT + t, :], ident16[:, :])
                last.then_inc(xt_ready, 1)

            def scores(c, i, buf=0):
                pe.wait_ge(xt_copied, c + 1)
                for t in range(CT):
                    dst = score[:, t % TH, i * CB + t // TH, :]
                    for k, (a, b) in enumerate(((0, 0), (0, 1), (1, 0))):
                        last = nc.tensor.matmul(dst, xt[:, buf, t, a, :], gws[:, b, :], start=(k == 0), stop=(k == 2))
                last.then_inc(scored, 1)

            def turn_probs(ph):
                pe.wait_ge(probs_ready, ph + 1)
                for h in range(TH):
                    last = nc.tensor.transpose(side[0:RW, h * P:(h + 1) * P],
                                               probs[:, h * HB:(h + 1) * HB, :].rearrange("p b e -> p (b e)"), ident[:, :])
                last.then_inc(pt_turned, 1)

            def turn_topk(ph):
                pe.wait_ge(topk_ready, ph + 1)
                for k, m in enumerate((idx2, top2)):
                    last = nc.tensor.transpose(side[:, k * RW:(k + 1) * RW], m[:, :, :].rearrange("r a s -> r (a s)"),
                                               ident[0:RW, 0:RW])
                last.then_inc(topk_turned, 1)

            def turn_onehot(p, b, k):
                pe.wait_ge(onehot_ready, p * HB + b + 1)
                dst = ps[:, Y_BANK + k, :].bitcast(FP16).rearrange("p (h q s) -> p h q s", h=TH, q=PAIRS)
                for h in range(TH):
                    for q in range(PAIRS):
                        last = nc.tensor.transpose(dst[:, h, q, :], onehot[:, b, q, h * P:(h + 1) * P], ident16[:, :])
                last.then_inc(turned, 1)

            def gather(p, b, k):
                pe.wait_ge(turned_copied, p * HB + b + 1)
                pe.wait_ge(high_copied, p * HB + b + 1)
                pe.wait_ge(low_copied, p * HB + b + 1)
                for part in range(2):
                    for h in range(TH):
                        last = nc.tensor.matmul(ps[:, 2 * k + part, :], xn[:, part, b * TH + h, :], onehot_t[:, k, h, :],
                                                start=(h == 0), stop=(h == TH - 1))
                last.then_inc(gathered, 1)

            def up(p, i, u):
                n = p * UNITS + i * 4 + u
                pe.wait_ge(gelu_done, n + 1)
                e = i * 2 + u // 2
                for j in range(2):
                    cols = slice((2 * (u % 2) + j) * P, (2 * (u % 2) + j + 1) * P)
                    for k, (a, b) in enumerate(((0, 0), (0, 1), (1, 0))):
                        last = nc.tensor.matmul(ps[:, 2 * (u % 2) + j, :], w1s[:, a, e, cols],
                                                xin[:, b, e, :, :].rearrange("p b s -> p (b s)"),
                                                start=(k == 0), stop=(k == 2))
                last.then_inc(up_done, 1)

            def down(p, i, u):
                n = p * UNITS + i * 4 + u
                e = i * 2 + u // 2
                pe.wait_ge(h_low, H_CREDIT + n + 1)
                if u % 2 == 0:
                    pe.wait_ge(y_copied, p * E + e + 1)
                for j in range(2):
                    for k, (a, b) in enumerate(((0, 0), (1, 0), (0, 1))):
                        last = nc.tensor.matmul(ps[:, Y_BANK, :], w2s[:, a, e, 2 * (u % 2) + j, :],
                                                hs[:, u, b, j * SLOTS:(j + 1) * SLOTS],
                                                start=(u % 2 == 0 and j == 0 and k == 0), stop=(u % 2 == 1 and j == 1 and k == 2))
                if u % 2 == 1:
                    last.then_inc(down_done, 1)

            def turn_y(p, i, g, bank=TY_BANK):
                n = (p * PAIRS + i) * 2 + g
                pe.wait_ge(y_copied, 1 + p * E + i * 2 + 2)
                if bank != Y_BANK:
                    pe.wait_ge(y_weighed, n + 1)
                for b in range(4):
                    last = nc.tensor.transpose(ps[:, bank, b * P:(b + 1) * P], yt[:, 4 * g + b, :, :].rearrange("p a s -> p (a s)"), ident[:, :])
                last.then_inc(y_turned, 1)

            def scatter(p, b, k, pairs):
                if 0 in pairs and p < NPH - 1:
                    pe.wait_ge(o_copied, p * HB + b + 1)
                for h in range(TH):
                    for q in pairs:
                        for part in range(2):
                            last = nc.tensor.matmul(ps[:, k, h * C:(h + 1) * C], onehot[:, b, q, h * P:(h + 1) * P],
                                                    ys[:, part, b, q, :], start=(h == 0 and q == 0 and part == 0),
                                                    stop=(h == TH - 1 and q == PAIRS - 1 and part == 1))
                if PAIRS - 1 in pairs:
                    last.then_inc(scattered, 1)

            pe.wait_ge(consts, 3)
            pe.wait_ge(gate_split, 1)
            for i in range(NCH):
                if i >= 2:
                    scores(i - 2, i - 2, i % 2)
                xn_turn(i, i, i % 2)
            for i in range(NCH - 2, NCH):
                scores(i, i, i % 2)
            pe.wait_ge(w2_in, 16)
            for e in range(E):
                if e == 1:
                    turn_probs(0)
                for k in range(HC):
                    last = nc.tensor.matmul(gram, w2f[:, e, k, :], w2f[:, e, k, :], start=(e == 0 and k == 0),
                                            stop=(e == E - 1 and k == HC - 1))
            last.then_inc(w2_gram, 1)
            turn_topk(0)
            for p in range(NPH):
                turn_onehot(p, 0, 0)
                with pe.Fori(0, HB // 2 - 1) as i:
                    turn_onehot(p, 2 * i + 1, 1)
                    gather(p, 2 * i, 0)
                    turn_onehot(p, 2 * i + 2, 0)
                    gather(p, 2 * i + 1, 1)
                turn_onehot(p, HB - 1, 1)
                gather(p, HB - 2, 0)
                gather(p, HB - 1, 1)

                att, nxt = (p - 1) * NCH, (p + 1) * NCH
                with_att, with_ffn = p in (1, 2), p < NPH - 1
                pe.wait_ge(high_copied, CREDIT + (p + 1) * HB)
                pe.wait_ge(low_copied, CREDIT + (p + 1) * HB)
                pe.wait_ge(w1_split, 1)
                up(p, 0, 0)
                if with_att:
                    pe.wait_ge(att_in, 6 * 16)
                    att_turn(att)
                up(p, 0, 1)
                if with_att:
                    att_in_proj(att)
                up(p, 0, 2)
                up(p, 0, 3)
                if with_att:
                    att_out_proj(att)
                pe.wait_ge(w2_split, 1)
                down(p, 0, 0)
                with pe.Fori(0, PAIRS - 1) as i:
                    up(p, i + 1, 0)
                    down(p, i, 1)
                    if with_att:
                        pe.wait_ge(v_added, att + i + 1)
                        pe.wait_ge(y_weighed, CREDIT + (p * PAIRS + i) * 2)
                        att_turn(att + i + 1)
                    up(p, i + 1, 1)
                    if with_att:
                        att_in_proj(att + i + 1)
                    down(p, i, 2)
                    up(p, i + 1, 2)
                    if with_ffn:
                        xn_turn(nxt + i, i, p=p)
                    if with_att:
                        att_out_proj(att + i + 1)
                    down(p, i, 3)
                    up(p, i + 1, 3)
                    if with_ffn:
                        scores(nxt + i, i)
                    turn_y(p, i, 0)
                    if with_att:
                        pe.wait_ge(v_added, att + i + 2)
                    turn_y(p, i, 1, SIDE_BANK)
                    down(p, i + 1, 0)
                down(p, PAIRS - 1, 1)
                down(p, PAIRS - 1, 2)
                if with_ffn:
                    xn_turn(nxt + NCH - 1, NCH - 1)
                pe.wait_ge(y_split, CREDIT + p * PAIRS * 2 + 2 * (PAIRS - 1))
                for b in range(2):
                    scatter(p, b, b, range(PAIRS - 1))
                if with_ffn:
                    scores(nxt + NCH - 1, NCH - 1)
                down(p, PAIRS - 1, 3)
                scatter(p, 2, 2, range(PAIRS - 1))
                if with_ffn:
                    turn_probs(p + 1)
                turn_y(p, PAIRS - 1, 0)
                turn_y(p, PAIRS - 1, 1, Y_BANK)
                scatter(p, 3, 3, range(PAIRS - 1))

                if with_ffn:
                    pe.wait_ge(y_split, CREDIT + p * PAIRS * 2 + 2 * (PAIRS - 1) + 1)
                    for b in range(HB // 2):
                        scatter(p, b, b, range(PAIRS - 1, PAIRS))
                    pe.wait_ge(y_split, CREDIT + (p + 1) * PAIRS * 2)
                    for b in range(HB // 2, HB):
                        scatter(p, b, b - HB // 2, range(PAIRS))
                else:
                    for b in range(4, 6):
                        scatter(p, b, FINAL_BANKS[b], range(PAIRS - 1))
                    for b in range(6):
                        pe.wait_ge(y_final, b // 4 + 1)
                        scatter(p, b, FINAL_BANKS[b], range(PAIRS - 1, PAIRS))
                    for b in range(6, HB):
                        pe.wait_ge(x_final, b - 5)
                        scatter(p, b, FINAL_BANKS[b], range(PAIRS))
                if with_ffn:
                    turn_topk(p + 1)


_INS = ['L0_attn_x', 'L0_attn_W_in', 'L0_attn_b_in', 'L0_attn_log_A', 'L0_attn_B_vec', 'L0_attn_C', 'L0_attn_D',
        'L0_ffn_gate_w', 'L0_ffn_w1', 'L0_ffn_w2']


def kernel(**inputs):
    import numpy as _np
    import concourse.bacc as _bacc
    from concourse import mybir as _mybir
    from concourse.bass_utils import run_bass_kernel_spmd as _run

    nc = _bacc.Bacc("TRN2", target_bir_lowering=False, num_devices=1)
    arrays, args = {}, []
    for name in _INS:
        a = _np.ascontiguousarray(inputs[name])
        arrays[f"in_{name}_dram"] = a
        args.append(nc.dram_tensor(f"in_{name}_dram", a.shape, _mybir.dt.from_np(a.dtype), kind="ExternalInput").ap())
    shape = inputs['L0_attn_x'].shape
    out = nc.dram_tensor("out_dram", shape, _mybir.dt.float32, kind="ExternalOutput").ap()
    macaron_kernel(nc, *args, out)
    r = _run(nc, [arrays], core_ids=[0])
    return r.results[0]["out_dram"]
```
